# Optimizing a Trainium2 kernel written in Bass

```python
import numpy as np
import jax
import jax.numpy as jnp

def _softmax(x, axis=-1):
    return jax.nn.softmax(x, axis=axis)

def _gelu(x):
    return jax.nn.gelu(x, approximate=True)

def _silu(x):
    return jax.nn.silu(x)

def _sigmoid(x):
    return jax.nn.sigmoid(x)

def _layernorm(x, axis=-1, eps=1e-05):
    m = jnp.mean(x, axis=axis, keepdims=True)
    v = jnp.var(x, axis=axis, keepdims=True)
    return (x - m) / jnp.sqrt(v + eps)

def _scatter_add(tgt, idx, src, axis=0):
    return tgt.at[idx].add(src)

def _segment_sum(src, seg, n):
    return jax.ops.segment_sum(src, seg, n)
kernel_name = 'mk_dlrm_tower_d1_rec_r8_418a2e'

def setup_inputs(seed: int=0):
    np.random.seed(seed)
    _w = jnp.asarray

    def _rec_inputs():
        import jax
        import jax.numpy as jnp
        _tk = jax.random.key(seed)
        dense_ctx = jax.random.normal(jax.random.fold_in(_tk, 190), (2048, 16), jnp.float32)
        ids = jnp.stack([jax.random.randint(jax.random.fold_in(_tk, 200 + f), (2048,), 0, v, jnp.int32) for f, v in enumerate([1000, 125000, 12500, 1000, 1000, 1250, 125000, 125000, 12500, 1000, 125000, 12500, 1250, 12500, 1250, 125000, 1250, 12500, 1000, 1250, 1000, 1000, 12500, 125000, 12500, 12500, 125000, 1000, 12500, 1250, 1000, 1250])], axis=1)
        tbl_0 = 0.05 * jax.random.normal(jax.random.fold_in(_tk, 500 + 0), (1000, 16), jnp.float32)
        tbl_1 = 0.05 * jax.random.normal(jax.random.fold_in(_tk, 500 + 1), (125000, 16), jnp.float32)
        tbl_2 = 0.05 * jax.random.normal(jax.random.fold_in(_tk, 500 + 2), (12500, 16), jnp.float32)
        tbl_3 = 0.05 * jax.random.normal(jax.random.fold_in(_tk, 500 + 3), (1000, 16), jnp.float32)
        tbl_4 = 0.05 * jax.random.normal(jax.random.fold_in(_tk, 500 + 4), (1000, 16), jnp.float32)
        tbl_5 = 0.05 * jax.random.normal(jax.random.fold_in(_tk, 500 + 5), (1250, 16), jnp.float32)
        tbl_6 = 0.05 * jax.random.normal(jax.random.fold_in(_tk, 500 + 6), (125000, 16), jnp.float32)
        tbl_7 = 0.05 * jax.random.normal(jax.random.fold_in(_tk, 500 + 7), (125000, 16), jnp.float32)
        tbl_8 = 0.05 * jax.random.normal(jax.random.fold_in(_tk, 500 + 8), (12500, 16), jnp.float32)
        tbl_9 = 0.05 * jax.random.normal(jax.random.fold_in(_tk, 500 + 9), (1000, 16), jnp.float32)
        tbl_10 = 0.05 * jax.random.normal(jax.random.fold_in(_tk, 500 + 10), (125000, 16), jnp.float32)
        tbl_11 = 0.05 * jax.random.normal(jax.random.fold_in(_tk, 500 + 11), (12500, 16), jnp.float32)
        tbl_12 = 0.05 * jax.random.normal(jax.random.fold_in(_tk, 500 + 12), (1250, 16), jnp.float32)
        tbl_13 = 0.05 * jax.random.normal(jax.random.fold_in(_tk, 500 + 13), (12500, 16), jnp.float32)
        tbl_14 = 0.05 * jax.random.normal(jax.random.fold_in(_tk, 500 + 14), (1250, 16), jnp.float32)
        tbl_15 = 0.05 * jax.random.normal(jax.random.fold_in(_tk, 500 + 15), (125000, 16), jnp.float32)
        tbl_16 = 0.05 * jax.random.normal(jax.random.fold_in(_tk, 500 + 16), (1250, 16), jnp.float32)
        tbl_17 = 0.05 * jax.random.normal(jax.random.fold_in(_tk, 500 + 17), (12500, 16), jnp.float32)
        tbl_18 = 0.05 * jax.random.normal(jax.random.fold_in(_tk, 500 + 18), (1000, 16), jnp.float32)
        tbl_19 = 0.05 * jax.random.normal(jax.random.fold_in(_tk, 500 + 19), (1250, 16), jnp.float32)
        tbl_20 = 0.05 * jax.random.normal(jax.random.fold_in(_tk, 500 + 20), (1000, 16), jnp.float32)
        tbl_21 = 0.05 * jax.random.normal(jax.random.fold_in(_tk, 500 + 21), (1000, 16), jnp.float32)
        tbl_22 = 0.05 * jax.random.normal(jax.random.fold_in(_tk, 500 + 22), (12500, 16), jnp.float32)
        tbl_23 = 0.05 * jax.random.normal(jax.random.fold_in(_tk, 500 + 23), (125000, 16), jnp.float32)
        tbl_24 = 0.05 * jax.random.normal(jax.random.fold_in(_tk, 500 + 24), (12500, 16), jnp.float32)
        tbl_25 = 0.05 * jax.random.normal(jax.random.fold_in(_tk, 500 + 25), (12500, 16), jnp.float32)
        tbl_26 = 0.05 * jax.random.normal(jax.random.fold_in(_tk, 500 + 26), (125000, 16), jnp.float32)
        tbl_27 = 0.05 * jax.random.normal(jax.random.fold_in(_tk, 500 + 27), (1000, 16), jnp.float32)
        tbl_28 = 0.05 * jax.random.normal(jax.random.fold_in(_tk, 500 + 28), (12500, 16), jnp.float32)
        tbl_29 = 0.05 * jax.random.normal(jax.random.fold_in(_tk, 500 + 29), (1250, 16), jnp.float32)
        tbl_30 = 0.05 * jax.random.normal(jax.random.fold_in(_tk, 500 + 30), (1000, 16), jnp.float32)
        tbl_31 = 0.05 * jax.random.normal(jax.random.fold_in(_tk, 500 + 31), (1250, 16), jnp.float32)
        _rk = jax.random.fold_in(_tk, 7)
        W_top1 = 0.0693375 * jax.random.normal(jax.random.fold_in(_tk, 801), (208, 512), jnp.float32)
        W_top2 = 0.0441942 * jax.random.normal(jax.random.fold_in(_tk, 802), (512, 256), jnp.float32)
        W_top3 = 0.0625 * jax.random.normal(jax.random.fold_in(_tk, 803), (256, 1), jnp.float32)
        b_top1 = jnp.zeros((512,), jnp.float32)
        b_top2 = jnp.zeros((256,), jnp.float32)
        return (dense_ctx, ids, tbl_0, tbl_1, tbl_2, tbl_3, tbl_4, tbl_5, tbl_6, tbl_7, tbl_8, tbl_9, tbl_10, tbl_11, tbl_12, tbl_13, tbl_14, tbl_15, tbl_16, tbl_17, tbl_18, tbl_19, tbl_20, tbl_21, tbl_22, tbl_23, tbl_24, tbl_25, tbl_26, tbl_27, tbl_28, tbl_29, tbl_30, tbl_31, W_top1, b_top1, W_top2, b_top2, W_top3)
    dense_ctx, ids, tbl_0, tbl_1, tbl_2, tbl_3, tbl_4, tbl_5, tbl_6, tbl_7, tbl_8, tbl_9, tbl_10, tbl_11, tbl_12, tbl_13, tbl_14, tbl_15, tbl_16, tbl_17, tbl_18, tbl_19, tbl_20, tbl_21, tbl_22, tbl_23, tbl_24, tbl_25, tbl_26, tbl_27, tbl_28, tbl_29, tbl_30, tbl_31, W_top1, b_top1, W_top2, b_top2, W_top3 = _rec_inputs()

    def _L0_rec_setup():
        import jax, jax.numpy as jnp
        import numpy as np
        B, M, D = (2048, 32, 16)
        LAYERS = [64, 64, 64]
        key = jax.random.key(seed)
        ks = jax.random.split(key, 4)
        inp = {'embeddings': jax.random.normal(ks[0], (B, M, D), dtype=jnp.float32)}
        hk_1 = M
        for i, hk in enumerate(LAYERS):
            scale = (2.0 / (M * hk_1 + hk)) ** 0.5
            inp[f'W{i}'] = jax.random.normal(ks[i + 1], (M, hk_1, hk), dtype=jnp.float32) * scale
            hk_1 = hk
        return inp
    _L0_rec_all = _L0_rec_setup()
    _L0_rec_in = {k: v for k, v in _L0_rec_all.items() if k in ('W0', 'W1', 'W2')}
    del _L0_rec_all
    return {'dense_ctx': dense_ctx, 'ids': ids, 'tbl_0': tbl_0, 'tbl_1': tbl_1, 'tbl_2': tbl_2, 'tbl_3': tbl_3, 'tbl_4': tbl_4, 'tbl_5': tbl_5, 'tbl_6': tbl_6, 'tbl_7': tbl_7, 'tbl_8': tbl_8, 'tbl_9': tbl_9, 'tbl_10': tbl_10, 'tbl_11': tbl_11, 'tbl_12': tbl_12, 'tbl_13': tbl_13, 'tbl_14': tbl_14, 'tbl_15': tbl_15, 'tbl_16': tbl_16, 'tbl_17': tbl_17, 'tbl_18': tbl_18, 'tbl_19': tbl_19, 'tbl_20': tbl_20, 'tbl_21': tbl_21, 'tbl_22': tbl_22, 'tbl_23': tbl_23, 'tbl_24': tbl_24, 'tbl_25': tbl_25, 'tbl_26': tbl_26, 'tbl_27': tbl_27, 'tbl_28': tbl_28, 'tbl_29': tbl_29, 'tbl_30': tbl_30, 'tbl_31': tbl_31, 'W_top1': W_top1, 'b_top1': b_top1, 'W_top2': W_top2, 'b_top2': b_top2, 'W_top3': W_top3, 'L0_rec_W0': _L0_rec_in['W0'], 'L0_rec_W1': _L0_rec_in['W1'], 'L0_rec_W2': _L0_rec_in['W2']}

def reference(dense_ctx, ids, tbl_0, tbl_1, tbl_2, tbl_3, tbl_4, tbl_5, tbl_6, tbl_7, tbl_8, tbl_9, tbl_10, tbl_11, tbl_12, tbl_13, tbl_14, tbl_15, tbl_16, tbl_17, tbl_18, tbl_19, tbl_20, tbl_21, tbl_22, tbl_23, tbl_24, tbl_25, tbl_26, tbl_27, tbl_28, tbl_29, tbl_30, tbl_31, W_top1, b_top1, W_top2, b_top2, W_top3, L0_rec_W0, L0_rec_W1, L0_rec_W2):
    import jax
    import jax.numpy as jnp

    def _L0_rec_ref(embeddings, W0, W1, W2):
        import jax, jax.numpy as jnp
        import numpy as np
        B, M, D = (2048, 32, 16)
        LAYERS = [64, 64, 64]
        x0 = embeddings
        xk = x0
        outs = []
        for W in (W0, W1, W2):
            xk = jax.nn.relu(jnp.einsum('bmd,bhd,mhk->bkd', x0, xk, W))
            outs.append(jnp.sum(xk, axis=2))
        return jnp.concatenate(outs, axis=1)
    e = jnp.stack([tbl_0[ids[:, 0]], tbl_1[ids[:, 1]], tbl_2[ids[:, 2]], tbl_3[ids[:, 3]], tbl_4[ids[:, 4]], tbl_5[ids[:, 5]], tbl_6[ids[:, 6]], tbl_7[ids[:, 7]], tbl_8[ids[:, 8]], tbl_9[ids[:, 9]], tbl_10[ids[:, 10]], tbl_11[ids[:, 11]], tbl_12[ids[:, 12]], tbl_13[ids[:, 13]], tbl_14[ids[:, 14]], tbl_15[ids[:, 15]], tbl_16[ids[:, 16]], tbl_17[ids[:, 17]], tbl_18[ids[:, 18]], tbl_19[ids[:, 19]], tbl_20[ids[:, 20]], tbl_21[ids[:, 21]], tbl_22[ids[:, 22]], tbl_23[ids[:, 23]], tbl_24[ids[:, 24]], tbl_25[ids[:, 25]], tbl_26[ids[:, 26]], tbl_27[ids[:, 27]], tbl_28[ids[:, 28]], tbl_29[ids[:, 29]], tbl_30[ids[:, 30]], tbl_31[ids[:, 31]]], axis=1)
    z = _L0_rec_ref(e, L0_rec_W0, L0_rec_W1, L0_rec_W2)
    z = z.reshape(z.shape[0], -1)
    h = jnp.concatenate([z, dense_ctx], axis=1)
    h = jnp.maximum(h @ W_top1 + b_top1, 0.0)
    h = jnp.maximum(h @ W_top2 + b_top2, 0.0)
    y = h @ W_top3
    return y

_drawn_inputs = setup_inputs


def setup_inputs(seed=0):
    import zlib

    import numpy as np

    out = dict(_drawn_inputs(seed))
    spreads = {'b_top1': (0.0, 2.0), 'b_top2': (0.0, 0.8)}
    factors = {'tbl_0': 8.0,
     'tbl_1': 8.0,
     'tbl_2': 8.0,
     'tbl_3': 8.0,
     'tbl_4': 8.0,
     'tbl_5': 8.0,
     'tbl_6': 8.0,
     'tbl_7': 8.0,
     'tbl_8': 8.0,
     'tbl_9': 8.0,
     'tbl_10': 8.0,
     'tbl_11': 8.0,
     'tbl_12': 8.0,
     'tbl_13': 8.0,
     'tbl_14': 8.0,
     'tbl_15': 8.0,
     'tbl_16': 8.0,
     'tbl_17': 8.0,
     'tbl_18': 8.0,
     'tbl_19': 8.0,
     'tbl_20': 8.0,
     'tbl_21': 8.0,
     'tbl_22': 8.0,
     'tbl_23': 8.0,
     'tbl_24': 8.0,
     'tbl_25': 8.0,
     'tbl_26': 8.0,
     'tbl_27': 8.0,
     'tbl_28': 8.0,
     'tbl_29': 8.0,
     'tbl_30': 8.0,
     'tbl_31': 8.0,
     'L0_rec_W0': 3.591,
     'L0_rec_W1': 8.0,
     'L0_rec_W2': 8.0,
     'dense_ctx': 7.664}
    for name, (base, spread) in spreads.items():
        noise = np.random.default_rng([zlib.crc32(name.encode()), seed]).standard_normal(out[name].shape)
        drawn = base * np.exp(spread * noise) if base else spread * noise
        out[name] = jnp.asarray(drawn.astype(out[name].dtype))
    for name, factor in factors.items():
        out[name] = (out[name] * factor).astype(out[name].dtype)
    return out
```

```python
from contextlib import ExitStack

import concourse.bass as bass
from concourse import mybir
import numpy as np

ALU = mybir.AluOpType
ACT = mybir.ActivationFunctionType
AX_X = mybir.AxisListType.X
F32 = mybir.dt.float32
BF16 = mybir.dt.bfloat16
I32 = mybir.dt.int32

P = 128
FIELDS = 32
DIM = 16
K = 64
BATCH = 2048
TILES = BATCH // P
SD = DIM // 2
COLS = SD * P
BLK = COLS // 2
SHIFTS = P // FIELDS
C0 = 5
HALF = FIELDS // 2
C1 = FIELDS * K // P
SEL_COPIED = C1 + 1
SEL = SEL_COPIED + C0
H1, H2 = 512, 256
DENSE = 16

POOL_CHUNKS = tuple(c for c in range(C1) if c % 4 == 3)
DVE_L = C1 - len(POOL_CHUNKS)
DVE_STEP = 2 * DVE_L + C0
POOL_STEP = 2 * len(POOL_CHUNKS)
DVE_RING = 6
POOL_RING = 2
ONE_BF16 = np.uint16(0x3F80)
L1, L2 = "second layer", "third layer"
Q_AT = C1 // 2
SPREAD_AFTER_L1 = [(), (), (), (0,), (1,), (2,), (3,), (4,), (5,), (6,), (7,), (8,), (9,), (10,), (), (11,)]
SPREAD_AFTER_L0 = [(12,), (13,), (), (), ()]
SPREAD_AFTER_L2 = [(14 + c // 2,) if c % 2 == 0 else () for c in range(C1)]
MLP1_AFTER, MLP2_AFTER, MLP1_AT = 9, 12, 7
SUM_AFTER, SPLIT_AFTER = 8, 12
HI_AFTER = [range(0, 3), range(3, 6), range(6, 9), range(9, 12), range(12, 14), range(14, 16), (), ()]
LO_AFTER = [(), (), range(0, 2), range(2, 4), range(4, 7), range(7, 10), range(10, 13), range(13, 16)]


def dve_index(layer, c, prepare):
    if layer == L1:
        return c - c // 4
    return DVE_L + C0 * prepare + c - c // 4


def pool_index(layer, c):
    return c // 4 + (len(POOL_CHUNKS) if layer == L2 else 0)


def dve_before(s):
    return C0 + DVE_STEP * s


def first_layer_from(s, first):
    return 0 if first else dve_before(s - 1) + DVE_L


def a_copied(s, c):
    return SEL_COPIED * s + (c + 1 if c < C1 // 2 else c + 2)


def build_kernel(nc, ids, tables, dense_t, w0_mh, w0_hm, w1, w2, w_top1, b_top1, w_top2, b_top2,
                 w_top3, sel_a, sel_r, ident, y):
    with ExitStack() as ctx:
        def sb(name, shape, dt=F32):
            return ctx.enter_context(nc.sbuf_tensor(name, shape, dt))

        def psum(name, shape, dt=F32):
            return ctx.enter_context(nc.psum_tensor(name, shape, dt))

        def sem(name):
            return ctx.enter_context(nc.semaphore(name))

        ids_lo = sb("ids_lo", [P, HALF], I32)
        ids_hi = sb("ids_hi", [P, HALF], I32)
        rows = sb("rows", [P, FIELDS * DIM])
        rest = sb("rest", [P, DIM, FIELDS])
        parts = sb("parts", [P, DIM, 3, FIELDS], BF16)
        x_parts = sb("x_parts", [3 * FIELDS, COLS], BF16)
        a_low = sb("a_low", [P, C1 // 2, COLS])
        a_high = sb("a_high", [P, 2, C1 // 2, COLS])
        q_tile = sb("q_tile", [P, COLS])
        x1 = sb("x1", [P, COLS])
        x2 = sb("x2", [P, COLS])
        p_dve = sb("p_dve", [P, DVE_RING, COLS])
        p_pool = sb("p_pool", [P, POOL_RING, COLS])
        out_l = sb("out_l", [P, 3, 2, BLK])
        z = sb("z", [P, 3, P])
        dense = sb("dense", [P, P])
        h1 = sb("h1", [P, H1 // P, P])
        h2 = sb("h2", [P, H2 // P, P])
        y_row = sb("y_row", [1, P])
        w0_a = sb("w0_a", [P, C0 - 1, K])
        w0_b = sb("w0_b", [P, C0 - 1, K])
        w0_s = sb("w0_s", [P, C0, K])
        w0_la = sb("w0_la", [HALF, K])
        w0_lb = sb("w0_lb", [HALF, K])
        w1_s = sb("w1_s", [P, C1, K])
        w2_s = sb("w2_s", [P, C1, K])
        wt1 = sb("wt1", [P, 3, H1])
        wt1_d = sb("wt1_d", [P, H1])
        wt2 = sb("wt2", [P, H1 // P, H2])
        wt3 = sb("wt3", [P, H2 // P])
        bt1 = sb("bt1", [P, H1 // P])
        bt2 = sb("bt2", [P, H2 // P])
        sel_as = sb("sel_as", [3 * FIELDS, FIELDS, K], BF16)
        sel_rs = sb("sel_rs", [3 * FIELDS, C0 + 1, P], BF16)
        idn = sb("idn", [P, P], BF16)

        acc = [psum(f"acc{n}", [P, BLK]) for n in range(3)]
        spread = psum("spread", [P, 2, COLS])
        aux = psum("aux", [P, COLS], BF16)
        aux_f = aux[:].bitcast(F32)

        w_loaded = sem("w_loaded")
        lo_loaded = sem("lo_loaded")
        hi_loaded = sem("hi_loaded")
        lo_gathered = sem("lo_gathered")
        hi_gathered = sem("hi_gathered")
        dense_loaded = sem("dense_loaded")
        y_stored = sem("y_stored")
        w0_ready = sem("w0_ready")
        split_step = sem("split_step")
        dense_clear = sem("dense_clear")
        dve_made = sem("dve_made")
        z_made = sem("z_made")
        pool_made = sem("pool_made")
        turned = sem("turned")
        spread_made = sem("spread_made")
        dve_used = sem("dve_used")
        pool_used = sem("pool_used")
        mlp_made = sem("mlp_made")
        x_copied = sem("x_copied")
        spread_copied = sem("spread_copied")
        relu_done = [sem(f"relu_done{n}") for n in range(3)]
        mlp_done = sem("mlp_done")


        CONSTS = [
            (idn[:], ident.bitcast(BF16)), (sel_rs[:], sel_r.bitcast(BF16)),
            (sel_as[:], sel_a.bitcast(BF16)),
            (w0_a[:], w0_mh[0:(C0 - 1) * P].rearrange("(c p) k -> p c k", p=P)),
            (w0_b[:], w0_hm[0:(C0 - 1) * P].rearrange("(c p) k -> p c k", p=P)),
            (w0_la[:], w0_mh[(C0 - 1) * P:]), (w0_lb[:], w0_hm[(C0 - 1) * P:]),
            (w1_s[:], w1.rearrange("(c p) k -> p c k", p=P)),
            (w2_s[:], w2.rearrange("(c p) k -> p c k", p=P)),
            (wt2[:], w_top2.rearrange("(c p) n -> p c n", p=P)),
            (wt3[:], w_top3), (bt1[:], b_top1), (bt2[:], b_top2),
        ] + [(wt1[b * K:(b + 1) * K, n, :], w_top1[n * K:(n + 1) * K])
             for n in range(3) for b in range(2)]
        LOADED = 16 * (len(CONSTS) + 1)

        def a_tile(u, layer, n):
            half = C1 // 2
            if (n < half) == (layer == L1):
                return a_high[:, u, n % half, :]
            return a_low[:, n % half, :]

        block = ctx.enter_context(nc.Block())

        @block.sync
        def _(sp):
            for dst, src in CONSTS:
                sp.dma_start(dst, src).then_inc(w_loaded, 16)
            sp.wait_ge(dense_clear, 2)
            sp.dma_start(wt1_d[0:DENSE, :], w_top1[3 * K:]).then_inc(w_loaded, 16)

            def tile(t, first):
                if not first:
                    sp.wait_ge(y_stored, 16 * t)
                sp.dma_start(dense[0:DENSE, :], dense_t[:, bass.ds(t * P, P)]).then_inc(dense_loaded, 16)
                sp.wait_ge(mlp_done, 3 * (t + 1))
                sp.dma_start(y[:, bass.ds(t * P, P)], y_row[:]).then_inc(y_stored, 16)

            tile(0, True)
            with sp.Fori(1, TILES) as t:
                tile(t, False)
            sp.wait_ge(y_stored, 16 * TILES)

        @block.gpsimd
        def _(pool):
            def load_lo(t, first=False):
                if not first:
                    pool.wait_ge(lo_gathered, 16 * HALF * t)
                pool.dma_start(ids_lo[:], ids[bass.ds(t * P, P), 0:HALF]).then_inc(lo_loaded, 16)

            def load_hi(t, first=False):
                if not first:
                    pool.wait_ge(hi_gathered, 16 * HALF * t)
                pool.dma_start(ids_hi[:], ids[bass.ds(t * P, P), HALF:FIELDS]).then_inc(hi_loaded, 16)

            def gather_lo(f):
                nc.gpsimd.indirect_dma_start(
                    out=rows[:, f * DIM:(f + 1) * DIM], out_offset=None, in_=tables[f],
                    in_offset=bass.IndirectOffsetOnAxis(ap=ids_lo[:, f:f + 1], axis=0),
                ).then_inc(lo_gathered, 16)

            def gather_hi(f):
                m = HALF + f
                nc.gpsimd.indirect_dma_start(
                    out=rows[:, m * DIM:(m + 1) * DIM], out_offset=None, in_=tables[m],
                    in_offset=bass.IndirectOffsetOnAxis(ap=ids_hi[:, f:f + 1], axis=0),
                ).then_inc(hi_gathered, 16)

            def product(s, u, first, layer, c):
                i = pool_index(layer, c)
                if i == 0:
                    pool.wait_ge(relu_done[0], s + 1)
                if i == len(POOL_CHUNKS):
                    pool.wait_ge(relu_done[1], s + 1)
                if layer == L1:
                    pool.wait_ge(spread_copied, a_copied(s, c))
                if not first or i >= POOL_RING:
                    pool.wait_ge(pool_used, POOL_STEP * s + i - POOL_RING + 1)
                x = x1 if layer == L1 else x2
                nc.gpsimd.tensor_tensor(p_pool[:, i % POOL_RING, :], a_tile(u, layer, c), x[:],
                                        ALU.mult).then_inc(pool_made, 1)

            def products(s, u, first, n):
                layer = L1 if n < len(POOL_CHUNKS) else L2
                product(s, u, first, layer, POOL_CHUNKS[n % len(POOL_CHUNKS)])

            def even_step(s, t, first, gather):
                if gather:
                    pool.wait_ge(hi_loaded, 16 * (t + 2))
                for n in range(POOL_STEP):
                    products(s, 0, first, n)
                    if gather:
                        for f in HI_AFTER[n]:
                            gather_hi(f)

            def odd_step(s, t, gather):
                if gather:
                    load_lo(t + 2)
                    load_hi(t + 2)
                for n in range(POOL_STEP):
                    if gather and LO_AFTER[n] and not LO_AFTER[n - 1]:
                        pool.wait_ge(lo_loaded, 16 * (t + 3))
                        pool.wait_ge(split_step, 4 * (t + 2))
                    products(s, 1, False, n)
                    if gather:
                        for f in LO_AFTER[n]:
                            gather_lo(f)

            load_lo(0, True)
            load_hi(0, True)
            pool.wait_ge(lo_loaded, 16)
            for f in range(HALF):
                gather_lo(f)
            pool.wait_ge(hi_loaded, 16)
            for f in range(HALF):
                gather_hi(f)
            load_lo(1)
            load_hi(1)
            pool.wait_ge(lo_loaded, 32)
            pool.wait_ge(split_step, 4)
            for f in range(HALF):
                gather_lo(f)
            even_step(0, 0, True, True)
            with pool.Fori(0, TILES - 2) as t:
                odd_step(2 * t + 1, t, True)
                even_step(2 * t + 2, t + 1, False, True)
            odd_step(2 * TILES - 3, TILES - 2, False)
            even_step(2 * TILES - 2, TILES - 1, False, False)
            odd_step(2 * TILES - 1, TILES - 1, False)

        @block.scalar
        def _(act):
            def copy_x(s, first):
                act.wait_ge(turned, s + 1)
                if not first:
                    act.wait_ge(spread_made, SEL * s)
                nc.scalar.activation(x_parts[:], aux[0:3 * FIELDS, :], ACT.Copy).then_inc(x_copied, 1)

            def copy_spread(s, u, j):
                act.wait_ge(spread_made, SEL * s + j + 1)
                dst = (a_high[:, u, j, :] if j < Q_AT else q_tile[:] if j == Q_AT
                       else a_low[:, j - Q_AT - 1 - C0, :])
                nc.scalar.activation(dst, spread[:, j % 2, :], ACT.Copy).then_inc(spread_copied, 1)

            def relu_both_halves(x, n):
                for b in range(2):
                    for half in range(2):
                        last = nc.scalar.activation(x[half * K:(half + 1) * K, b * BLK:(b + 1) * BLK],
                                                    acc[n][b * K:(b + 1) * K, :], ACT.Relu)
                return last

            def relu0(s, u, first, before):
                act.wait_ge(dve_used, first_layer_from(s, first) + C0)
                relu_both_halves(x1, 0)
                if u == 0 and not first:
                    act.wait_ge(z_made, 3 * before - 2)
                nc.scalar.activation(out_l[:, 0, u, :], acc[0][:], ACT.Relu).then_inc(relu_done[0], 1)

            def relu1(s, u, before):
                act.wait_ge(dve_used, dve_before(s) + DVE_L)
                act.wait_ge(pool_used, POOL_STEP * s + len(POOL_CHUNKS))
                relu_both_halves(x2, 1)
                if before is not None:
                    act.wait_ge(z_made, 3 * before)
                nc.scalar.activation(out_l[:, 1, u, :], acc[1][:], ACT.Relu).then_inc(relu_done[1], 1)

            def relu2(s, u, prepare, before):
                act.wait_ge(dve_used, dve_before(s) + 2 * DVE_L + C0 * prepare)
                act.wait_ge(pool_used, POOL_STEP * (s + 1))
                if before is not None:
                    act.wait_ge(z_made, 3 * before)
                nc.scalar.activation(out_l[:, 2, u, :], acc[2][:], ACT.Relu).then_inc(relu_done[2], 1)

            def mlp1(t):
                act.wait_ge(mlp_made, 3 * t + 1)
                for n in range(H1 // P):
                    last = nc.scalar.activation(h1[:, n, :], aux_f[:, n * P:(n + 1) * P], ACT.Relu,
                                                bias=bt1[:, n:n + 1])
                last.then_inc(mlp_done, 1)

            def mlp2(t):
                act.wait_ge(mlp_made, 3 * t + 2)
                for n in range(H2 // P):
                    last = nc.scalar.activation(h2[:, n, :], aux_f[:, n * P:(n + 1) * P], ACT.Relu,
                                                bias=bt2[:, n:n + 1])
                last.then_inc(mlp_done, 1)

            def mlp3(t):
                act.wait_ge(mlp_made, 3 * t + 3)
                nc.scalar.activation(y_row[:], aux_f[0:1, 0:P], ACT.Copy).then_inc(mlp_done, 1)

            def step(s, u, prepare, tile_before, sums_of_next):
                if prepare:
                    copy_x(s + 1, False)
                    for j in range(Q_AT):
                        if j == MLP1_AT and tile_before is not None:
                            mlp1(tile_before)
                        copy_spread(s + 1, 1 - u, j)
                    copy_spread(s + 1, 1 - u, Q_AT)
                    if tile_before is not None:
                        mlp2(tile_before)
                relu1(s, u, None if tile_before is None else tile_before + 1)
                if prepare:
                    if tile_before is not None:
                        mlp3(tile_before)
                    relu0(s + 1, 1 - u, False, sums_of_next)
                    for j in range(Q_AT + 1 + C0, SEL):
                        copy_spread(s + 1, 1 - u, j)
                relu2(s, u, prepare, None if tile_before is None else tile_before + 1)

            act.wait_ge(w_loaded, LOADED)
            copy_x(0, True)
            for j in range(Q_AT + 1):
                copy_spread(0, 0, j)
            relu0(0, 0, True, None)
            for j in range(Q_AT + 1 + C0, SEL):
                copy_spread(0, 0, j)
            step(0, 0, True, None, None)
            with act.Fori(0, TILES - 1) as t:
                step(2 * t + 1, 1, True, None, t + 1)
                step(2 * t + 2, 0, True, t, None)
            step(2 * TILES - 1, 1, False, None, None)
            mlp1(TILES - 1)
            mlp2(TILES - 1)
            mlp3(TILES - 1)

        @block.vector
        def _(dve):
            def slot_free(s, i, first):
                if i >= DVE_RING:
                    dve.wait_ge(dve_used, dve_before(s) + i - DVE_RING + 1)
                else:
                    j = i + DVE_RING * ((DVE_STEP - 1 - i) // DVE_RING)
                    if not first or i < C0:
                        dve.wait_ge(dve_used, dve_before(s) - DVE_STEP + j + 1)

            def product(s, u, first, prepare, layer, c):
                i = dve_index(layer, c, prepare)
                slot_free(s, i, first)
                if i == 0:
                    dve.wait_ge(relu_done[0], s + 1)
                if c == 0 and layer == L2:
                    dve.wait_ge(relu_done[1], s + 1)
                if layer == L1:
                    dve.wait_ge(spread_copied, a_copied(s, c))
                x = x1 if layer == L1 else x2
                nc.vector.tensor_tensor(p_dve[:, i % DVE_RING, :], a_tile(u, layer, c), x[:],
                                        ALU.mult).then_inc(dve_made, 1)

            def first_layer_product(s, first, c, slot):
                n = P if c < C0 - 1 else HALF
                if c == 0:
                    dve.wait_ge(spread_copied, SEL_COPIED * s + Q_AT + 1)
                dve.wait_ge(spread_made, SEL * s + Q_AT + 2 + c)
                nc.vector.tensor_tensor(p_dve[0:n, slot, :], spread[0:n, (Q_AT + 1 + c) % 2, :],
                                        q_tile[0:n, :], ALU.mult).then_inc(dve_made, 1)

            def split(t, first):
                dve.wait_ge(lo_gathered, 16 * HALF * (t + 1))
                dve.wait_ge(hi_gathered, 16 * HALF * (t + 1))
                if not first:
                    dve.wait_ge(turned, 2 * t)
                full = rows[:].rearrange("p (m d) -> p d m", d=DIM)
                nc.vector.tensor_copy(parts[:, :, 0, :], full).then_inc(split_step, 1)
                dve.wait_ge(split_step, 4 * t + 1)
                nc.vector.tensor_tensor(rest[:], full, parts[:, :, 0, :], ALU.subtract).then_inc(split_step, 1)
                dve.wait_ge(split_step, 4 * t + 2)
                nc.vector.tensor_copy(parts[:, :, 1, :], rest[:]).then_inc(split_step, 1)
                dve.wait_ge(split_step, 4 * t + 3)
                nc.vector.tensor_tensor(parts[:, :, 2, :], rest[:], parts[:, :, 1, :],
                                        ALU.subtract).then_inc(split_step, 1)

            def sums(t, n):
                dve.wait_ge(relu_done[n], 2 * (t + 1))
                nc.vector.reduce_sum(z[:, n, :], out_l[:, n, :, :].rearrange("p u (d b) -> p b (u d)", b=P),
                                     AX_X).then_inc(z_made, 1)

            def step(s, u, first, prepare, this, before, nxt):
                for c in range(C1):
                    if c in POOL_CHUNKS:
                        continue
                    product(s, u, first, prepare, L1, c)
                    if c == SUM_AFTER and before is not None:
                        sums(before, 2)
                    if c == SUM_AFTER and this is not None:
                        sums(this, 0)
                if prepare:
                    for c in range(C0):
                        slot_free(s, DVE_L + c, first)
                        first_layer_product(s + 1, False, c, (DVE_L + c) % DVE_RING)
                for c in range(C1):
                    if c in POOL_CHUNKS:
                        continue
                    product(s, u, first, prepare, L2, c)
                    if c == SUM_AFTER and this is not None:
                        sums(this, 1)
                    if c == SPLIT_AFTER and nxt is not None:
                        split(nxt, False)

            nc.vector.memset(dense[:], 0.0).then_inc(dense_clear, 1)
            nc.vector.memset(wt1_d[:], 0.0).then_inc(dense_clear, 1)
            split(0, True)
            dve.wait_ge(w_loaded, LOADED)
            nc.vector.tensor_tensor(w0_s[:, 0:C0 - 1, :], w0_a[:], w0_b[:], ALU.add).then_inc(w0_ready, 1)
            nc.vector.tensor_tensor(w0_s[0:HALF, C0 - 1, :], w0_la[:], w0_lb[:], ALU.add).then_inc(w0_ready, 1)
            dve.wait_ge(w0_ready, 2)
            nc.vector.tensor_copy(w0_s[0:FIELDS, 0, :], w0_a[0:FIELDS, 0, :]).then_inc(w0_ready, 1)
            for c in range(C0):
                first_layer_product(0, True, c, c)
            step(0, 0, True, True, None, None, 1)
            with dve.Fori(0, TILES - 2) as t:
                step(2 * t + 1, 1, False, True, t, None, None)
                step(2 * t + 2, 0, False, True, None, t, t + 2)
            step(2 * TILES - 3, 1, False, True, TILES - 2, None, None)
            step(2 * TILES - 2, 0, False, True, None, TILES - 2, None)
            step(2 * TILES - 1, 1, False, False, TILES - 1, None, None)
            sums(TILES - 1, 2)

        @block.tensor
        def _(pe):
            def turn(s, u, first):
                if u == 0:
                    pe.wait_ge(split_step, 2 * s + 4)
                if not first:
                    pe.wait_ge(x_copied, s)
                for d in range(SD):
                    last = nc.tensor.transpose(aux[0:3 * FIELDS, d * P:(d + 1) * P],
                                               parts[:, u * SD + d, :, :].rearrange("p a m -> p (a m)"),
                                               idn[:])
                last.then_inc(turned, 1)

            def spread_x(s, j, first):
                if j == 0:
                    pe.wait_ge(x_copied, s + 1)
                n = j - 2
                if Q_AT < n <= Q_AT + C0:
                    pe.wait_ge(dve_made, first_layer_from(s, first) + n - Q_AT)
                elif not first or n >= 0:
                    pe.wait_ge(spread_copied, SEL_COPIED * s + n + 1 - (C0 if n > Q_AT else 0))
                for r in range(2):
                    if j == Q_AT or Q_AT < j <= Q_AT + C0:
                        w = sel_rs[:, j - Q_AT, r * K:(r + 1) * K]
                    else:
                        w = sel_as[:, 2 * (j + C1 // 2 if j < Q_AT else j - Q_AT - 1 - C0) + r, :]
                    if j == Q_AT + C0 and r == 1:
                        continue
                    for b in range(2):
                        last = nc.tensor.matmul(spread[r * K:(r + 1) * K, j % 2, b * BLK:(b + 1) * BLK],
                                                w, x_parts[:, b * BLK:(b + 1) * BLK], start=True, stop=True)
                last.then_inc(spread_made, 1)

            def contract(n, w, prod, start, stop):
                for b in range(2):
                    last = nc.tensor.matmul(acc[n][b * K:(b + 1) * K, :], w,
                                            prod[:, b * BLK:(b + 1) * BLK], start=start, stop=stop)
                return last

            def chunk(s, prepare, layer, c):
                n, w = (1, w1_s[:, (c + C1 // 2) % C1, :]) if layer == L1 else (2, w2_s[:, c, :])
                if c == 0:
                    pe.wait_ge(relu_done[n], s)
                if c in POOL_CHUNKS:
                    i = pool_index(layer, c)
                    pe.wait_ge(pool_made, POOL_STEP * s + i + 1)
                    contract(n, w, p_pool[:, i % POOL_RING, :], c == 0, c == C1 - 1
                             ).then_inc(pool_used, 1)
                else:
                    i = dve_index(layer, c, prepare)
                    pe.wait_ge(dve_made, dve_before(s) + i + 1)
                    contract(n, w, p_dve[:, i % DVE_RING, :], c == 0, c == C1 - 1
                             ).then_inc(dve_used, 1)

            def first_layer_chunk(s, first, c, slot):
                n = P if c < C0 - 1 else HALF
                if c == 0 and not first:
                    pe.wait_ge(relu_done[0], s)
                pe.wait_ge(dve_made, first_layer_from(s, first) + c + 1)
                contract(0, w0_s[0:n, c, :], p_dve[0:n, slot, :], c == 0, c == C0 - 1
                         ).then_inc(dve_used, 1)

            def mlp1(t):
                pe.wait_ge(z_made, 3 * (t + 1))
                pe.wait_ge(dense_loaded, 16 * (t + 1))
                for n in range(H1 // P):
                    cols = slice(n * P, (n + 1) * P)
                    for k in range(3):
                        nc.tensor.matmul(aux_f[:, cols], wt1[:, k, cols], z[:, k, :],
                                         start=(k == 0), stop=False)
                    last = nc.tensor.matmul(aux_f[:, cols], wt1_d[:, cols], dense[:],
                                            start=False, stop=True)
                last.then_inc(mlp_made, 1)

            def mlp2(t):
                pe.wait_ge(mlp_done, 3 * t + 1)
                for n in range(H2 // P):
                    cols = slice(n * P, (n + 1) * P)
                    for k in range(H1 // P):
                        last = nc.tensor.matmul(aux_f[:, cols], wt2[:, k, cols], h1[:, k, :],
                                                start=(k == 0), stop=(k == H1 // P - 1))
                last.then_inc(mlp_made, 1)

            def mlp3(t):
                pe.wait_ge(mlp_done, 3 * t + 2)
                for k in range(H2 // P):
                    last = nc.tensor.matmul(aux_f[0:1, 0:P], wt3[:, k:k + 1], h2[:, k, :],
                                            start=(k == 0), stop=(k == H2 // P - 1))
                last.then_inc(mlp_made, 1)

            def step(s, u, prepare, before):
                for c in range(C1):
                    chunk(s, prepare, L1, c)
                    if prepare:
                        if c == 0:
                            turn(s + 1, 1 - u, False)
                        for j in SPREAD_AFTER_L1[c]:
                            spread_x(s + 1, j, False)
                        if before is not None and c == MLP1_AFTER:
                            mlp1(before)
                        if before is not None and c == MLP2_AFTER:
                            mlp2(before)
                if prepare:
                    if before is not None:
                        mlp3(before)
                    for c in range(C0):
                        first_layer_chunk(s + 1, False, c, (DVE_L + c) % DVE_RING)
                        for j in SPREAD_AFTER_L0[c]:
                            spread_x(s + 1, j, False)
                for c in range(C1):
                    chunk(s, prepare, L2, c)
                    if prepare:
                        for j in SPREAD_AFTER_L2[c]:
                            spread_x(s + 1, j, False)
                if before is not None:
                    pe.wait_ge(mlp_done, 3 * (before + 1))

            pe.wait_ge(w_loaded, LOADED)
            turn(0, 0, True)
            for j in range(Q_AT + 1 + C0):
                spread_x(0, j, True)
            pe.wait_ge(w0_ready, 3)
            for c in range(C0):
                first_layer_chunk(0, True, c, c)
            for j in range(Q_AT + 1 + C0, SEL):
                spread_x(0, j, True)
            step(0, 0, True, None)
            with pe.Fori(0, TILES - 1) as t:
                step(2 * t + 1, 1, True, None)
                step(2 * t + 2, 0, True, t)
            step(2 * TILES - 1, 1, False, None)
            mlp1(TILES - 1)
            mlp2(TILES - 1)
            mlp3(TILES - 1)


def pairs():
    delta, m = np.divmod(np.arange(FIELDS * HALF), FIELDS)
    delta = np.concatenate([delta, np.full(HALF, HALF)])
    m = np.concatenate([m, np.arange(HALF)])
    return m, (m + delta) % FIELDS


def selectors():
    of = np.tile(np.arange(FIELDS), 3)[:, None]
    field = np.repeat(np.arange(FIELDS), K)[None, :]
    p = np.arange(P)
    shifted = [p % FIELDS] + [(p % FIELDS + SHIFTS * c + p // FIELDS) % FIELDS for c in range(C0)]
    r = np.concatenate(shifted)[None, :]
    return ((of == field).astype(np.uint16).reshape(3 * FIELDS, FIELDS, K) * ONE_BF16,
            (of == r).astype(np.uint16).reshape(3 * FIELDS, C0 + 1, P) * ONE_BF16)


def kernel(**inputs):
    import concourse.bacc as bacc
    from concourse.bass_utils import run_bass_kernel_spmd

    raw = {k: np.asarray(v) for k, v in inputs.items()}
    m, h = pairs()
    w0 = raw["L0_rec_W0"]
    sel_a, sel_r = selectors()
    arrays = {"ids": raw["ids"]}
    arrays.update({f"tbl_{f}": raw[f"tbl_{f}"] for f in range(FIELDS)})
    arrays.update(
        dense_t=raw["dense_ctx"].T, w0_mh=w0[m, h], w0_hm=w0[h, m],
        w1=raw["L0_rec_W1"].reshape(FIELDS * K, K), w2=raw["L0_rec_W2"].reshape(FIELDS * K, K),
        w_top1=raw["W_top1"], b_top1=raw["b_top1"].reshape(H1 // P, P).T,
        w_top2=raw["W_top2"], b_top2=raw["b_top2"].reshape(H2 // P, P).T,
        w_top3=raw["W_top3"].reshape(H2 // P, P).T,
        sel_a=sel_a, sel_r=sel_r, ident=np.eye(P, dtype=np.uint16) * ONE_BF16,
    )
    arrays = {f"in_{k}": np.ascontiguousarray(v) for k, v in arrays.items()}

    nc = bacc.Bacc("TRN2", target_bir_lowering=False, num_devices=1)
    aps = {k[3:]: nc.dram_tensor(k, v.shape, mybir.dt.from_np(v.dtype), kind="ExternalInput").ap()
           for k, v in arrays.items()}
    tables = [aps.pop(f"tbl_{f}") for f in range(FIELDS)]
    y = nc.dram_tensor("y", (1, BATCH), F32, kind="ExternalOutput").ap()
    build_kernel(nc, tables=tables, y=y, **aps)
    result = run_bass_kernel_spmd(nc, [arrays], core_ids=[0])
    return result.results[0]["y"].reshape(BATCH, 1)
```

```python
from contextlib import ExitStack

import concourse.bass as bass
from concourse import mybir
import numpy as np

ALU = mybir.AluOpType
ACT = mybir.ActivationFunctionType
AX_X = mybir.AxisListType.X
F32 = mybir.dt.float32
BF16 = mybir.dt.bfloat16
I32 = mybir.dt.int32

P = 128
FIELDS = 32
DIM = 16
K = 64
BATCH = 2048
TILES = BATCH // P
SD = DIM // 2
COLS = SD * P
BLK = COLS // 2
SHIFTS = P // FIELDS
C0 = 5
HALF = FIELDS // 2
C1 = FIELDS * K // P
SEL = 1 + C0
GROUP = 4
H1, H2 = 512, 256
DENSE = 16

POOL_CHUNKS = tuple(c for c in range(C1) if c % 4 == 3)
DVE_L = C1 - len(POOL_CHUNKS)
DVE_STEP = 2 * DVE_L + C0
POOL_STEP = 2 * len(POOL_CHUNKS)
DVE_RING = 6
POOL_RING = 3
ONE_BF16 = np.uint16(0x3F80)
L1, L2 = "second layer", "third layer"
TURN_AFTER = (0, 3)
SPREAD_AFTER = {2: 0, 3: 1, 4: 2, 5: 3, 7: 4, 8: 5}
R_KEPT = 3
COPIED = 1 + R_KEPT
MLP1_AFTER, MLP2_AFTER = 9, 13
SUM_AFTER, SPLIT_AFTER = 8, 14
HI_AFTER = [range(0, 3), range(3, 6), range(6, 9), range(9, 12), range(12, 14), range(14, 16), (), ()]
LO_AFTER = [range(2 * n, 2 * n + 2) for n in range(8)]


def dve_index(layer, c, prepare):
    if layer == L1:
        return c - c // 4
    return DVE_L + C0 * prepare + c - c // 4


def pool_index(layer, c):
    return c // 4 + (len(POOL_CHUNKS) if layer == L2 else 0)


def dve_before(s):
    return C0 + DVE_STEP * s


def first_layer_from(s, first):
    return 0 if first else dve_before(s - 1) + DVE_L


def last_in_buffer(i, ring, per_step):
    return i - ring if i >= ring else i + ring * ((per_step - 1 - i) // ring) - per_step


def a_loads(s, u):
    return 16 * (s - u) + 32


def build_kernel(nc, ids, tables, dense_t, w0_mh, w0_hm, w1, w2, w_top1, b_top1, w_top2, b_top2,
                 w_top3, sel_r, ident, scratch, y):
    with ExitStack() as ctx:
        def sb(name, shape, dt=F32):
            return ctx.enter_context(nc.sbuf_tensor(name, shape, dt))

        def psum(name, shape, dt=F32):
            return ctx.enter_context(nc.psum_tensor(name, shape, dt))

        def sem(name):
            return ctx.enter_context(nc.semaphore(name))

        ids_lo = sb("ids_lo", [P, HALF], I32)
        ids_hi = sb("ids_hi", [P, HALF], I32)
        rows = sb("rows", [P, FIELDS * DIM])
        rest = sb("rest", [P, DIM, FIELDS])
        parts = sb("parts", [P, DIM, 3, FIELDS], BF16)
        x_parts = sb("x_parts", [3 * FIELDS, COLS], BF16)
        a_low = sb("a_low", [P, C1 // 2, COLS])
        a_high = sb("a_high", [P, 2, C1 // 2, COLS])
        q_tile = sb("q_tile", [P, COLS])
        r_tiles = sb("r_tiles", [P, R_KEPT, COLS])
        x1 = sb("x1", [P, COLS])
        x2 = sb("x2", [P, COLS])
        p_dve = sb("p_dve", [P, DVE_RING, COLS])
        p_pool = sb("p_pool", [P, POOL_RING, COLS])
        out_l = sb("out_l", [P, 3, 2, BLK])
        z = sb("z", [P, 3, P])
        dense = sb("dense", [P, P])
        h1 = sb("h1", [P, H1 // P, P])
        h2 = sb("h2", [P, H2 // P, P])
        y_row = sb("y_row", [1, P])
        w0_b = sb("w0_b", [P, C0 - 1, K])
        w0_s = sb("w0_s", [P, C0, K])
        w0_lb = sb("w0_lb", [HALF, K])
        w1_s = sb("w1_s", [P, C1, K])
        w2_s = sb("w2_s", [P, C1, K])
        wt1 = sb("wt1", [P, 3, H1])
        wt1_d = sb("wt1_d", [P, H1])
        wt2 = sb("wt2", [P, H1 // P, H2])
        wt3 = sb("wt3", [P, H2 // P])
        bt1 = sb("bt1", [P, H1 // P])
        bt2 = sb("bt2", [P, H2 // P])
        sel_rs = sb("sel_rs", [3 * FIELDS, SEL, P], BF16)
        idn = sb("idn", [P, P], BF16)

        acc = [psum(f"acc{n}", [P, BLK]) for n in range(3)]
        spread = psum("spread", [P, 2, COLS])
        aux = psum("aux", [P, COLS], BF16)
        aux_f = aux[:].bitcast(F32)

        w_loaded = sem("w_loaded")
        lo_loaded = sem("lo_loaded")
        hi_loaded = sem("hi_loaded")
        lo_gathered = sem("lo_gathered")
        hi_gathered = sem("hi_gathered")
        dense_loaded = sem("dense_loaded")
        x_stored = sem("x_stored")
        a_loaded = [[sem(f"a_loaded{u}{g}") for g in range(C1 // GROUP)] for u in range(2)]
        y_stored = sem("y_stored")
        w0_ready = sem("w0_ready")
        split_step = sem("split_step")
        dense_clear = sem("dense_clear")
        dve_made = sem("dve_made")
        z_made = sem("z_made")
        pool_made = sem("pool_made")
        turned = sem("turned")
        spread_made = sem("spread_made")
        dve_used = sem("dve_used")
        pool_used = sem("pool_used")
        mlp_made = sem("mlp_made")
        x_copied = sem("x_copied")
        spread_copied = sem("spread_copied")
        relu_done = [sem(f"relu_done{n}") for n in range(3)]
        x_ready = [sem(f"x{n + 1}_ready") for n in range(2)]
        mlp_done = sem("mlp_done")


        CONSTS = [
            (idn[:], ident.bitcast(BF16)), (sel_rs[:], sel_r.bitcast(BF16)),
            (w0_s[:, 0:C0 - 1, :], w0_mh[0:(C0 - 1) * P].rearrange("(c p) k -> p c k", p=P)),
            (w0_b[:], w0_hm[0:(C0 - 1) * P].rearrange("(c p) k -> p c k", p=P)),
            (w0_s[0:HALF, C0 - 1, :], w0_mh[(C0 - 1) * P:]), (w0_lb[:], w0_hm[(C0 - 1) * P:]),
            (w1_s[:], w1.rearrange("(c p) k -> p c k", p=P)),
            (w2_s[:], w2.rearrange("(c p) k -> p c k", p=P)),
            (wt2[:], w_top2.rearrange("(c p) n -> p c n", p=P)),
            (wt3[:], w_top3), (bt1[:], b_top1), (bt2[:], b_top2),
        ] + [(wt1[b * K:(b + 1) * K, n, :], w_top1[n * K:(n + 1) * K])
             for n in range(3) for b in range(2)]
        LOADED = 16 * (len(CONSTS) + 1)

        def a_tile(u, layer, n):
            half = C1 // 2
            if (n < half) == (layer == L1):
                return a_high[:, u, n % half, :]
            return a_low[:, n % half, :]

        block = ctx.enter_context(nc.Block())

        @block.sync
        def _(sp):
            for dst, src in CONSTS:
                sp.dma_start(dst, src).then_inc(w_loaded, 16)
            sp.wait_ge(dense_clear, 2)
            sp.dma_start(wt1_d[0:DENSE, :], w_top1[3 * K:]).then_inc(w_loaded, 16)

            def load_a(u, g):
                c = (g * GROUP + C1 // 2) % C1
                x0 = scratch[u].rearrange("(c r) n -> r c n", r=2)
                for r in range(2):
                    place = slice(r * K, (r + 1) * K), slice(c % (C1 // 2), c % (C1 // 2) + GROUP)
                    dst = a_low[place[0], place[1], :] if c < C1 // 2 else a_high[place[0], u, place[1], :]
                    src = x0[r:r + 1, c:c + GROUP, :].broadcast_to([K, GROUP, COLS])
                    sp.dma_start(dst, src).then_inc(a_loaded[u][g], 16)

            def step(s, u):
                sp.wait_ge(spread_copied, COPIED * (s + 1) + 1)
                sp.dma_start(scratch[1 - u], q_tile[0:FIELDS, :]).then_inc(x_stored, 16)
                sp.wait_ge(x_stored, 16 * (s + 2))
                load_a(1 - u, 0)
                load_a(1 - u, 1)
                for g in range(2):
                    sp.wait_ge(pool_used, POOL_STEP * s + pool_index(L2, g * GROUP + GROUP - 1) + 1)
                    load_a(1 - u, 2 + g)

            sp.wait_ge(spread_copied, 1)
            sp.dma_start(scratch[0], q_tile[0:FIELDS, :]).then_inc(x_stored, 16)
            sp.wait_ge(x_stored, 16)
            for g in range(C1 // GROUP):
                load_a(0, g)
            step(0, 0)
            with sp.Fori(0, TILES - 1) as t:
                step(2 * t + 1, 1)
                step(2 * t + 2, 0)

        @block.gpsimd
        def _(pool):
            def load_lo(t, first=False):
                if not first:
                    pool.wait_ge(lo_gathered, 16 * HALF * t)
                pool.dma_start(ids_lo[:], ids[bass.ds(t * P, P), 0:HALF]).then_inc(lo_loaded, 16)

            def load_hi(t, first=False):
                if not first:
                    pool.wait_ge(hi_gathered, 16 * HALF * t)
                pool.dma_start(ids_hi[:], ids[bass.ds(t * P, P), HALF:FIELDS]).then_inc(hi_loaded, 16)

            def gather_lo(f):
                nc.gpsimd.indirect_dma_start(
                    out=rows[:, f * DIM:(f + 1) * DIM], out_offset=None, in_=tables[f],
                    in_offset=bass.IndirectOffsetOnAxis(ap=ids_lo[:, f:f + 1], axis=0),
                ).then_inc(lo_gathered, 16)

            def gather_hi(f):
                m = HALF + f
                nc.gpsimd.indirect_dma_start(
                    out=rows[:, m * DIM:(m + 1) * DIM], out_offset=None, in_=tables[m],
                    in_offset=bass.IndirectOffsetOnAxis(ap=ids_hi[:, f:f + 1], axis=0),
                ).then_inc(hi_gathered, 16)

            def product(s, u, first, layer, c):
                i = pool_index(layer, c)
                if i == 0:
                    pool.wait_ge(x_ready[0], s + 1)
                if i == len(POOL_CHUNKS):
                    pool.wait_ge(x_ready[1], s + 1)
                if layer == L1:
                    pool.wait_ge(a_loaded[u][c // GROUP], a_loads(s, u))
                if not first or i >= POOL_RING:
                    pool.wait_ge(pool_used, POOL_STEP * s + last_in_buffer(i, POOL_RING, POOL_STEP) + 1)
                x = x1 if layer == L1 else x2
                nc.gpsimd.tensor_tensor(p_pool[:, i % POOL_RING, :], a_tile(u, layer, c), x[:],
                                        ALU.mult).then_inc(pool_made, 1)

            def products(s, u, first, n):
                layer = L1 if n < len(POOL_CHUNKS) else L2
                product(s, u, first, layer, POOL_CHUNKS[n % len(POOL_CHUNKS)])

            def even_step(s, t, first, gather):
                if gather:
                    pool.wait_ge(hi_loaded, 16 * (t + 2))
                for n in range(POOL_STEP):
                    products(s, 0, first, n)
                    if gather:
                        for f in HI_AFTER[n]:
                            gather_hi(f)

            def odd_step(s, t, gather):
                if gather:
                    load_lo(t + 2)
                    load_hi(t + 2)
                for n in range(POOL_STEP):
                    if gather and n == 0:
                        pool.wait_ge(lo_loaded, 16 * (t + 3))
                        pool.wait_ge(split_step, 4 * (t + 2))
                    products(s, 1, False, n)
                    if gather:
                        for f in LO_AFTER[n]:
                            gather_lo(f)

            load_lo(0, True)
            load_hi(0, True)
            pool.wait_ge(lo_loaded, 16)
            for f in range(HALF):
                gather_lo(f)
            pool.wait_ge(hi_loaded, 16)
            for f in range(HALF):
                gather_hi(f)
            load_lo(1)
            load_hi(1)
            pool.wait_ge(lo_loaded, 32)
            pool.wait_ge(split_step, 4)
            for f in range(HALF):
                gather_lo(f)
            even_step(0, 0, True, True)
            with pool.Fori(0, TILES - 2) as t:
                odd_step(2 * t + 1, t, True)
                even_step(2 * t + 2, t + 1, False, True)
            odd_step(2 * TILES - 3, TILES - 2, False)
            even_step(2 * TILES - 2, TILES - 1, False, False)
            odd_step(2 * TILES - 1, TILES - 1, False)

        @block.scalar
        def _(act):
            def copy_x(s, first):
                act.wait_ge(turned, s + 1)
                if not first:
                    act.wait_ge(spread_made, SEL * s)
                nc.scalar.activation(x_parts[:], aux[0:3 * FIELDS, :], ACT.Copy).then_inc(x_copied, 1)

            def copy_spread(s, first):
                for j in range(COPIED):
                    act.wait_ge(spread_made, SEL * s + j + 1)
                    if j == 0 and not first:
                        act.wait_ge(x_stored, 16 * s)
                    dst = r_tiles[:, j - 1, :] if j > 0 else q_tile[:]
                    nc.scalar.activation(dst, spread[:, j % 2, :], ACT.Copy).then_inc(spread_copied, 1)

            def relu_both_halves(x, n):
                for b in range(2):
                    for half in range(2):
                        last = nc.scalar.activation(x[half * K:(half + 1) * K, b * BLK:(b + 1) * BLK],
                                                    acc[n][b * K:(b + 1) * K, :], ACT.Relu)
                last.then_inc(x_ready[n], 1)

            def relu0(s, u, first, before):
                act.wait_ge(dve_used, first_layer_from(s, first) + C0)
                relu_both_halves(x1, 0)
                if u == 0 and not first:
                    act.wait_ge(z_made, 3 * before - 2)
                nc.scalar.activation(out_l[:, 0, u, :], acc[0][:], ACT.Relu).then_inc(relu_done[0], 1)

            def relu1(s, u, before):
                act.wait_ge(dve_used, dve_before(s) + DVE_L)
                act.wait_ge(pool_used, POOL_STEP * s + len(POOL_CHUNKS))
                relu_both_halves(x2, 1)
                if before is not None:
                    act.wait_ge(z_made, 3 * before)
                nc.scalar.activation(out_l[:, 1, u, :], acc[1][:], ACT.Relu).then_inc(relu_done[1], 1)

            def relu2(s, u, prepare, before):
                act.wait_ge(dve_used, dve_before(s) + 2 * DVE_L + C0 * prepare)
                act.wait_ge(pool_used, POOL_STEP * (s + 1))
                if before is not None:
                    act.wait_ge(z_made, 3 * before)
                nc.scalar.activation(out_l[:, 2, u, :], acc[2][:], ACT.Relu).then_inc(relu_done[2], 1)

            def mlp1(t):
                act.wait_ge(mlp_made, 3 * t + 1)
                for n in range(H1 // P):
                    last = nc.scalar.activation(h1[:, n, :], aux_f[:, n * P:(n + 1) * P], ACT.Relu,
                                                bias=bt1[:, n:n + 1])
                last.then_inc(mlp_done, 1)

            def mlp2(t):
                act.wait_ge(mlp_made, 3 * t + 2)
                for n in range(H2 // P):
                    last = nc.scalar.activation(h2[:, n, :], aux_f[:, n * P:(n + 1) * P], ACT.Relu,
                                                bias=bt2[:, n:n + 1])
                last.then_inc(mlp_done, 1)

            def mlp3(t):
                act.wait_ge(mlp_made, 3 * t + 3)
                nc.scalar.activation(y_row[:], aux_f[0:1, 0:P], ACT.Copy).then_inc(mlp_done, 1)
                act.wait_ge(mlp_done, 3 * t + 3)
                act.dma_start(y[:, bass.ds(t * P, P)], y_row[:]).then_inc(y_stored, 16)

            def load_dense(t):
                act.dma_start(dense[0:DENSE, :], dense_t[:, bass.ds(t * P, P)]).then_inc(dense_loaded, 16)

            def step(s, u, prepare, tile_before, sums_of_next):
                if tile_before is not None:
                    load_dense(tile_before)
                if prepare:
                    copy_x(s + 1, False)
                    copy_spread(s + 1, False)
                    if tile_before is not None:
                        mlp1(tile_before)
                        mlp2(tile_before)
                relu1(s, u, None if tile_before is None else tile_before + 1)
                if prepare:
                    if tile_before is not None:
                        mlp3(tile_before)
                    relu0(s + 1, 1 - u, False, sums_of_next)
                relu2(s, u, prepare, None if tile_before is None else tile_before + 1)
                if tile_before is not None:
                    act.wait_ge(y_stored, 16 * (tile_before + 1))

            act.wait_ge(w_loaded, LOADED)
            act.wait_ge(dense_clear, 2)
            copy_x(0, True)
            copy_spread(0, True)
            relu0(0, 0, True, None)
            step(0, 0, True, None, None)
            with act.Fori(0, TILES - 1) as t:
                step(2 * t + 1, 1, True, None, t + 1)
                step(2 * t + 2, 0, True, t, None)
            load_dense(TILES - 1)
            step(2 * TILES - 1, 1, False, None, None)
            mlp1(TILES - 1)
            mlp2(TILES - 1)
            mlp3(TILES - 1)
            act.wait_ge(y_stored, 16 * TILES)

        @block.vector
        def _(dve):
            def slot_free(s, i, first):
                if not first or i < C0 or i >= DVE_RING:
                    dve.wait_ge(dve_used, dve_before(s) + last_in_buffer(i, DVE_RING, DVE_STEP) + 1)

            def product(s, u, first, prepare, layer, c):
                i = dve_index(layer, c, prepare)
                slot_free(s, i, first)
                if i == 0:
                    dve.wait_ge(x_ready[0], s + 1)
                if c == 0 and layer == L2:
                    dve.wait_ge(x_ready[1], s + 1)
                if layer == L1 and c % GROUP == 0:
                    dve.wait_ge(a_loaded[u][c // GROUP], a_loads(s, u))
                x = x1 if layer == L1 else x2
                nc.vector.tensor_tensor(p_dve[:, i % DVE_RING, :], a_tile(u, layer, c), x[:],
                                        ALU.mult).then_inc(dve_made, 1)

            def first_layer_product(s, first, c, slot):
                n = P if c < C0 - 1 else HALF
                if c < R_KEPT:
                    dve.wait_ge(spread_copied, COPIED * s + 2 + c)
                    r = r_tiles[:, c, :]
                else:
                    dve.wait_ge(spread_made, SEL * s + 2 + c)
                    r = spread[0:n, (1 + c) % 2, :]
                nc.vector.tensor_tensor(p_dve[0:n, slot, :], r,
                                        q_tile[0:n, :], ALU.mult).then_inc(dve_made, 1)

            def split(t, first):
                dve.wait_ge(lo_gathered, 16 * HALF * (t + 1))
                dve.wait_ge(hi_gathered, 16 * HALF * (t + 1))
                if not first:
                    dve.wait_ge(turned, 2 * t)
                full = rows[:].rearrange("p (m d) -> p d m", d=DIM)
                nc.vector.tensor_copy(parts[:, :, 0, :], full).then_inc(split_step, 1)
                dve.wait_ge(split_step, 4 * t + 1)
                nc.vector.tensor_tensor(rest[:], full, parts[:, :, 0, :], ALU.subtract).then_inc(split_step, 1)
                dve.wait_ge(split_step, 4 * t + 2)
                nc.vector.tensor_copy(parts[:, :, 1, :], rest[:]).then_inc(split_step, 1)
                dve.wait_ge(split_step, 4 * t + 3)
                nc.vector.tensor_tensor(parts[:, :, 2, :], rest[:], parts[:, :, 1, :],
                                        ALU.subtract).then_inc(split_step, 1)

            def sums(t, n):
                dve.wait_ge(relu_done[n], 2 * (t + 1))
                nc.vector.reduce_sum(z[:, n, :], out_l[:, n, :, :].rearrange("p u (d b) -> p b (u d)", b=P),
                                     AX_X).then_inc(z_made, 1)

            def step(s, u, first, prepare, this, before, nxt):
                for c in range(C1):
                    if c in POOL_CHUNKS:
                        continue
                    product(s, u, first, prepare, L1, c)
                    if c == SUM_AFTER and before is not None:
                        sums(before, 2)
                    if c == SUM_AFTER and this is not None:
                        sums(this, 0)
                if prepare:
                    for c in range(C0):
                        slot_free(s, DVE_L + c, first)
                        first_layer_product(s + 1, False, c, (DVE_L + c) % DVE_RING)
                for c in range(C1):
                    if c in POOL_CHUNKS:
                        continue
                    product(s, u, first, prepare, L2, c)
                    if c == SUM_AFTER and this is not None:
                        sums(this, 1)
                    if c == SPLIT_AFTER and nxt is not None:
                        split(nxt, False)

            nc.vector.memset(dense[:], 0.0).then_inc(dense_clear, 1)
            nc.vector.memset(wt1_d[:], 0.0).then_inc(dense_clear, 1)
            split(0, True)
            dve.wait_ge(w_loaded, LOADED)
            for part in (w0_s[FIELDS:K, 0, :], w0_b[FIELDS:K, 0, :]), (w0_s[K:, 0, :], w0_b[K:, 0, :]), \
                    (w0_s[:, 1:C0 - 1, :], w0_b[:, 1:, :]), (w0_s[0:HALF, C0 - 1, :], w0_lb[:]):
                nc.vector.tensor_tensor(part[0], part[0], part[1], ALU.add).then_inc(w0_ready, 1)
            for c in range(C0):
                first_layer_product(0, True, c, c)
            step(0, 0, True, True, None, None, 1)
            with dve.Fori(0, TILES - 2) as t:
                step(2 * t + 1, 1, False, True, t, None, None)
                step(2 * t + 2, 0, False, True, None, t, t + 2)
            step(2 * TILES - 3, 1, False, True, TILES - 2, None, None)
            step(2 * TILES - 2, 0, False, True, None, TILES - 2, None)
            step(2 * TILES - 1, 1, False, False, TILES - 1, None, None)
            sums(TILES - 1, 2)

        @block.tensor
        def _(pe):
            def turn(s, u, first):
                if u == 0:
                    pe.wait_ge(split_step, 2 * s + 4)
                if not first:
                    pe.wait_ge(x_copied, s)
                for d in range(SD):
                    last = nc.tensor.transpose(aux[0:3 * FIELDS, d * P:(d + 1) * P],
                                               parts[:, u * SD + d, :, :].rearrange("p a m -> p (a m)"),
                                               idn[:])
                last.then_inc(turned, 1)

            def spread_x(s, j):
                if j == 0:
                    pe.wait_ge(x_copied, s + 1)
                if j >= 2:
                    pe.wait_ge(spread_copied, COPIED * s + j - 1)
                for r in range(1 if j == C0 else 2):
                    for b in range(2):
                        last = nc.tensor.matmul(spread[r * K:(r + 1) * K, j % 2, b * BLK:(b + 1) * BLK],
                                                sel_rs[:, j, r * K:(r + 1) * K],
                                                x_parts[:, b * BLK:(b + 1) * BLK], start=True, stop=True)
                last.then_inc(spread_made, 1)

            def contract(n, w, prod, start, stop):
                for b in range(2):
                    last = nc.tensor.matmul(acc[n][b * K:(b + 1) * K, :], w,
                                            prod[:, b * BLK:(b + 1) * BLK], start=start, stop=stop)
                return last

            def chunk(s, prepare, layer, c):
                n, w = (1, w1_s[:, (c + C1 // 2) % C1, :]) if layer == L1 else (2, w2_s[:, c, :])
                if c == 0:
                    pe.wait_ge(relu_done[n], s)
                if c in POOL_CHUNKS:
                    i = pool_index(layer, c)
                    pe.wait_ge(pool_made, POOL_STEP * s + i + 1)
                    contract(n, w, p_pool[:, i % POOL_RING, :], c == 0, c == C1 - 1
                             ).then_inc(pool_used, 1)
                else:
                    i = dve_index(layer, c, prepare)
                    pe.wait_ge(dve_made, dve_before(s) + i + 1)
                    contract(n, w, p_dve[:, i % DVE_RING, :], c == 0, c == C1 - 1
                             ).then_inc(dve_used, 1)

            def first_layer_chunk(s, first, c, slot):
                n = P if c < C0 - 1 else HALF
                if c == 0 and not first:
                    pe.wait_ge(relu_done[0], s)
                pe.wait_ge(dve_made, first_layer_from(s, first) + c + 1)
                contract(0, w0_s[0:n, c, :], p_dve[0:n, slot, :], c == 0, c == C0 - 1
                         ).then_inc(dve_used, 1)

            def mlp1(t):
                pe.wait_ge(z_made, 3 * (t + 1))
                pe.wait_ge(dense_loaded, 16 * (t + 1))
                for n in range(H1 // P):
                    cols = slice(n * P, (n + 1) * P)
                    for k in range(3):
                        nc.tensor.matmul(aux_f[:, cols], wt1[:, k, cols], z[:, k, :],
                                         start=(k == 0), stop=False)
                    last = nc.tensor.matmul(aux_f[:, cols], wt1_d[:, cols], dense[:],
                                            start=False, stop=True)
                last.then_inc(mlp_made, 1)

            def mlp2(t):
                pe.wait_ge(mlp_done, 3 * t + 1)
                for n in range(H2 // P):
                    cols = slice(n * P, (n + 1) * P)
                    for k in range(H1 // P):
                        last = nc.tensor.matmul(aux_f[:, cols], wt2[:, k, cols], h1[:, k, :],
                                                start=(k == 0), stop=(k == H1 // P - 1))
                last.then_inc(mlp_made, 1)

            def mlp3(t):
                pe.wait_ge(mlp_done, 3 * t + 2)
                for k in range(H2 // P):
                    last = nc.tensor.matmul(aux_f[0:1, 0:P], wt3[:, k:k + 1], h2[:, k, :],
                                            start=(k == 0), stop=(k == H2 // P - 1))
                last.then_inc(mlp_made, 1)

            def step(s, u, prepare, before):
                for c in range(C1):
                    chunk(s, prepare, L1, c)
                    if prepare:
                        if c == TURN_AFTER[u]:
                            turn(s + 1, 1 - u, False)
                        if c - TURN_AFTER[u] in SPREAD_AFTER:
                            spread_x(s + 1, SPREAD_AFTER[c - TURN_AFTER[u]])
                        if before is not None and c == MLP1_AFTER:
                            mlp1(before)
                        if before is not None and c == MLP2_AFTER:
                            mlp2(before)
                if prepare:
                    if before is not None:
                        mlp3(before)
                    for c in range(C0):
                        first_layer_chunk(s + 1, False, c, (DVE_L + c) % DVE_RING)
                for c in range(C1):
                    chunk(s, prepare, L2, c)
                if before is not None:
                    pe.wait_ge(mlp_done, 3 * (before + 1))

            pe.wait_ge(w_loaded, LOADED)
            turn(0, 0, True)
            for j in range(SEL):
                spread_x(0, j)
            pe.wait_ge(w0_ready, 4)
            for c in range(C0):
                first_layer_chunk(0, True, c, c)
            step(0, 0, True, None)
            with pe.Fori(0, TILES - 1) as t:
                step(2 * t + 1, 1, True, None)
                step(2 * t + 2, 0, True, t)
            step(2 * TILES - 1, 1, False, None)
            mlp1(TILES - 1)
            mlp2(TILES - 1)
            mlp3(TILES - 1)


def pairs():
    delta, m = np.divmod(np.arange(FIELDS * HALF), FIELDS)
    delta = np.concatenate([delta, np.full(HALF, HALF)])
    m = np.concatenate([m, np.arange(HALF)])
    return m, (m + delta) % FIELDS


def selector():
    p = np.arange(P)
    field = [p % FIELDS] + [(p % FIELDS + SHIFTS * c + p // FIELDS) % FIELDS for c in range(C0)]
    hot = np.tile(np.arange(FIELDS), 3)[:, None] == np.concatenate(field)[None, :]
    return hot.astype(np.uint16).reshape(3 * FIELDS, SEL, P) * ONE_BF16


def kernel(**inputs):
    import concourse.bacc as bacc
    from concourse.bass_utils import run_bass_kernel_spmd

    raw = {k: np.asarray(v) for k, v in inputs.items()}
    m, h = pairs()
    w0 = raw["L0_rec_W0"]
    arrays = {"ids": raw["ids"]}
    arrays.update({f"tbl_{f}": raw[f"tbl_{f}"] for f in range(FIELDS)})
    arrays.update(
        dense_t=raw["dense_ctx"].T, w0_mh=w0[m, h], w0_hm=w0[h, m],
        w1=raw["L0_rec_W1"].reshape(FIELDS * K, K), w2=raw["L0_rec_W2"].reshape(FIELDS * K, K),
        w_top1=raw["W_top1"], b_top1=raw["b_top1"].reshape(H1 // P, P).T,
        w_top2=raw["W_top2"], b_top2=raw["b_top2"].reshape(H2 // P, P).T,
        w_top3=raw["W_top3"].reshape(H2 // P, P).T,
        sel_r=selector(), ident=np.eye(P, dtype=np.uint16) * ONE_BF16,
    )
    arrays = {f"in_{k}": np.ascontiguousarray(v) for k, v in arrays.items()}

    nc = bacc.Bacc("TRN2", target_bir_lowering=False, num_devices=1)
    aps = {k[3:]: nc.dram_tensor(k, v.shape, mybir.dt.from_np(v.dtype), kind="ExternalInput").ap()
           for k, v in arrays.items()}
    tables = [aps.pop(f"tbl_{f}") for f in range(FIELDS)]
    y = nc.dram_tensor("y", (1, BATCH), F32, kind="ExternalOutput").ap()
    scratch = nc.dram_tensor("x0_of_two_steps", (2, FIELDS, COLS), F32, kind="Internal").ap()
    build_kernel(nc, tables=tables, scratch=scratch, y=y, **aps)
    result = run_bass_kernel_spmd(nc, [arrays], core_ids=[0])
    return result.results[0]["y"].reshape(BATCH, 1)
```

```python
from contextlib import ExitStack

import concourse.bass as bass
from concourse import mybir
import numpy as np

ALU = mybir.AluOpType
ACT = mybir.ActivationFunctionType
AX_X = mybir.AxisListType.X
F32 = mybir.dt.float32
I32 = mybir.dt.int32

P = 128
FIELDS = 32
DIM = 16
K = 64
BATCH = 2048
TILES = BATCH // P
SD = DIM // 2
COLS = SD * P
BLK = COLS // 2
SHIFTS = P // FIELDS
C0 = 5
HALF = FIELDS // 2
C1 = FIELDS * K // P
SPREAD = C1 // 2
TURNS = FIELDS * DIM // P
X_ROWS = 2 * FIELDS
GROUP = 4
H1, H2 = 512, 256
DENSE = 16
TOP = K + DENSE

ORDER_L1 = [(0, c) for c in range(SPREAD)] + [(1, c) for c in range(SPREAD)]
ORDER_L2 = ORDER_L1[:GROUP] + ORDER_L1[SPREAD:] + ORDER_L1[GROUP:SPREAD]
POOL_CHUNKS = tuple(c for c in range(C1) if c % 4 == 3)
DVE_L = C1 - len(POOL_CHUNKS)
DVE_STEP = 2 * DVE_L + C0
POOL_STEP = 2 * len(POOL_CHUNKS)
DVE_RING = 4
POOL_RING = 2
L0, L1, L2 = "first layer", "second layer", "third layer"
DVE_ORDER = ([(L1, c) for c in range(C1) if c not in POOL_CHUNKS] + [(L0, c) for c in range(C0)]
             + [(L2, c) for c in range(C1) if c not in POOL_CHUNKS])
DVE_GROUPS = [(0, 3), (4, 3), (8, 3), (12, 3)]
DVE_GROUPS_L2 = [(0, 1), (1, 1), (2, 1), (4, 1), (5, 2), (8, 1), (9, 2), (12, 3)]
TURN_AFTER = 4
COPY_AFTER = 2
MLP1_AFTER = 14
MLP2_AFTER, MLP3_AFTER = 1, 3
SUM_AFTER = 8
SUM1_AFTER, FOLD_AFTER = 4, 12
LO_EVEN, LO_ODD = 4, 16
HI = FIELDS - LO_EVEN - LO_ODD
LO = FIELDS - HI
LO_FROM = 6
HI_AFTER = [range(0, 1), range(1, 2), range(2, 3), range(3, 9), range(9, 12), (), (), ()]
LO_AFTER_EVEN = [(), (), (), (), (), (), range(0, 2), range(2, 4)]
LO_AFTER_ODD = [range(4, 5), range(5, 6), range(6, 7), range(7, 13), range(13, 14),
                range(14, 15), range(15, 17), range(17, 20)]


def dve_index(layer, c, prepare):
    if layer == L1:
        return c - c // 4
    return DVE_L + C0 * prepare + c - c // 4


def dve_buffer(u, layer, c):
    three = {L1: 0, L0: 4, L2: 6}[layer] + (c // 3 if layer == L0 else c // 4)
    return 3 * ((10 * u + three) % DVE_RING) + (c % 3 if layer == L0 else c % 4)


def dve_last_use(u, prepare, first, layer, c):
    before = [dve_buffer(1, L0, n) for n in range(C0)] if first else \
        [dve_buffer(v, *product) for v in (u, 1 - u) for product in DVE_ORDER]
    now = [dve_buffer(u, *product) for product in DVE_ORDER[:DVE_ORDER.index((layer, c))]
           if prepare or product[0] != L0]
    uses = [i for i, b in enumerate(before + now) if b == dve_buffer(u, layer, c)]
    return uses[-1] - len(before) if uses else None


def pool_index(layer, c):
    return c // 4 + (len(POOL_CHUNKS) if layer == L2 else 0)


def dve_before(s):
    return C0 + DVE_STEP * s


def first_layer_from(s, first):
    return 0 if first else dve_before(s - 1) + DVE_L


def last_in_buffer(i, ring, per_step):
    return i - ring if i >= ring else i + ring * ((per_step - 1 - i) // ring) - per_step


def build_kernel(nc, ids, tables, dense_t, w0_mh, w0_hm, w1, w2, w_top1, b_top1, w_top2, b_top2,
                 w_top3, ident, scratch, y):
    with ExitStack() as ctx:
        def sb(name, shape, dt=F32):
            return ctx.enter_context(nc.sbuf_tensor(name, shape, dt))

        def psum(name, shape, dt=F32):
            return ctx.enter_context(nc.psum_tensor(name, shape, dt))

        def sem(name):
            return ctx.enter_context(nc.semaphore(name))

        ids_lo = sb("ids_lo", [P, LO], I32)
        ids_hi = sb("ids_hi", [P, HI], I32)
        rows = sb("rows", [P, FIELDS * DIM])
        x_or_h1 = sb("x_or_h1", [P, H1])
        spread = sb("spread", [P, 2, SPREAD, COLS])
        swapped = sb("swapped", [P, SPREAD, COLS])
        q_tile = sb("q_tile", [P, COLS])
        x1 = sb("x1", [P, COLS])
        x2 = sb("x2", [P, COLS])
        p_dve = sb("p_dve", [P, 3 * DVE_RING, COLS])
        p_pool = sb("p_pool", [P, POOL_RING, COLS])
        out_l = sb("out_l", [P, 3, 2, BLK])
        z = sb("z", [P, 3, P])
        z_moved = sb("z_moved", [P, 2, P])
        z_all = sb("z_all", [P, 2, P])
        h2 = sb("h2", [P, H2 // P, P])
        y_row = sb("y_row", [1, P])
        w0_b = sb("w0_b", [P, C0 - 1, K])
        w0_s = sb("w0_s", [P, C0, K])
        w0_lb = sb("w0_lb", [HALF, K])
        w1_s = sb("w1_s", [P, C1, K])
        w2_s = sb("w2_s", [P, C1, K])
        wt1 = sb("wt1", [P, 2, H1])
        wt2 = sb("wt2", [P, H1 // P, H2])
        wt3 = sb("wt3", [P, H2 // P])
        bt1 = sb("bt1", [P, H1 // P])
        bt2 = sb("bt2", [P, H2 // P])
        idn = sb("idn", [P, P])

        acc = [psum(f"acc{n}", [P, BLK]) for n in range(3)]
        turned_x = psum("turned_x", [P, TURNS, P])
        mlp_acc = psum("mlp_acc", [P, H1])
        x_tile = x_or_h1[:].rearrange("p (j b) -> p j b", b=P)
        h1 = x_or_h1[:].rearrange("p (n b) -> p n b", b=P)

        w_loaded = sem("w_loaded")
        lo_loaded = sem("lo_loaded")
        hi_loaded = sem("hi_loaded")
        lo_gathered = sem("lo_gathered")
        hi_gathered = sem("hi_gathered")
        dense_loaded = sem("dense_loaded")
        x_stored = sem("x_stored")
        q_loaded = sem("q_loaded")
        spread_loaded = [sem(f"spread_loaded{g}") for g in range(SPREAD // GROUP)]
        y_stored = sem("y_stored")
        w0_ready = sem("w0_ready")
        dve_made = sem("dve_made")
        z_summed = sem("z_summed")
        z_made = sem("z_made")
        pool_made = sem("pool_made")
        turned = sem("turned")
        dve_used = sem("dve_used")
        pool_used = sem("pool_used")
        mlp_made = sem("mlp_made")
        x_copied = sem("x_copied")
        swap_done = sem("swap_done")
        relu_done = [sem(f"relu_done{n}") for n in range(3)]
        x_ready = [sem(f"x{n + 1}_ready") for n in range(2)]
        z_moved_ready = sem("z_moved_ready")
        mlp_done = sem("mlp_done")


        CONSTS = [
            (idn[:], ident),
            (w0_s[:, 0:C0 - 1, :], w0_mh[0:(C0 - 1) * P].rearrange("(c p) k -> p c k", p=P)),
            (w0_b[:], w0_hm[0:(C0 - 1) * P].rearrange("(c p) k -> p c k", p=P)),
            (w0_s[0:HALF, C0 - 1, :], w0_mh[(C0 - 1) * P:]), (w0_lb[:], w0_hm[(C0 - 1) * P:]),
            (w1_s[:], w1.rearrange("(c p) k -> p c k", p=P)),
            (w2_s[:], w2.rearrange("(c p) k -> p c k", p=P)),
            (wt2[:], w_top2.rearrange("(c p) n -> p c n", p=P)),
            (wt3[:], w_top3), (bt1[:], b_top1), (bt2[:], b_top2),
            (wt1[:, 0, :], w_top1[0:P]), (wt1[0:TOP, 1, :], w_top1[P:]),
        ]
        LOADED = 16 * len(CONSTS)

        def a_tile(u, layer, n):
            half_swapped, c = (ORDER_L1 if layer == L1 else ORDER_L2)[n]
            return swapped[:, c, :] if half_swapped else spread[:, u, c, :]

        block = ctx.enter_context(nc.Block())

        @block.sync
        def _(sp):
            for dst, src in CONSTS:
                sp.dma_start(dst, src).then_inc(w_loaded, 16)

            def x0_of(t, u, a, b):
                return scratch[bass.ds(t, 1), a:b, u * COLS:(u + 1) * COLS].rearrange("t m n -> (t m) n")

            def load_spread(t, u, g):
                for q in reversed(range(P // FIELDS)):
                    first = x0_of(t, u, SHIFTS * GROUP * g + q, SHIFTS * GROUP * g + q + 1)
                    src = bass.AP(first.tensor, first.offset,
                                  [[DIM * P, FIELDS], [SHIFTS * DIM * P, GROUP], [1, COLS]])
                    sp.dma_start(spread[q * FIELDS:(q + 1) * FIELDS, u, g * GROUP:(g + 1) * GROUP, :],
                                 src).then_inc(spread_loaded[g], 16)

            def load_q(t, u):
                first = x0_of(t, u, 0, 1)
                src = bass.AP(first.tensor, first.offset, [[0, P // FIELDS], [DIM * P, FIELDS], [1, COLS]])
                sp.dma_start(q_tile[:], src).then_inc(q_loaded, 16)

            def store_x(t):
                for first in 0, FIELDS:
                    dst = scratch[bass.ds(t, 1), first:first + FIELDS, :].rearrange(
                        "t (j m) (d b) -> (t m d) j b", j=TURNS, b=P)
                    sp.dma_start(dst, x_tile).then_inc(x_stored, 16)

            def step(s, u, t):
                if u == 0:
                    sp.wait_ge(x_copied, t + 2)
                    store_x(t + 1)
                    sp.wait_ge(x_stored, 32 * (t + 2))
                if u == 1:
                    sp.wait_ge(pool_used, POOL_STEP * s + pool_index(L2, GROUP - 1) + 1)
                load_spread(t + 1, u, 0)
                load_q(t + 1, u)
                sp.wait_ge(pool_used, POOL_STEP * (s + 1))
                load_spread(t + 1, u, 1)

            sp.wait_ge(x_copied, 1)
            store_x(0)
            sp.wait_ge(x_stored, 32)
            load_q(0, 0)
            load_spread(0, 0, 0)
            load_spread(0, 0, 1)
            sp.wait_ge(dve_used, C0)
            load_q(0, 1)
            load_spread(0, 1, 0)
            load_spread(0, 1, 1)
            step(0, 0, 0)
            with sp.Fori(0, TILES - 2) as t:
                step(2 * t + 1, 1, t)
                step(2 * t + 2, 0, t + 1)
            step(2 * TILES - 3, 1, TILES - 2)

        @block.gpsimd
        def _(pool):
            def load_lo(t, first=False):
                if not first:
                    pool.wait_ge(lo_gathered, 16 * LO * t)
                pool.dma_start(ids_lo[:], ids[bass.ds(t * P, P), 0:LO]).then_inc(lo_loaded, 16)

            def load_hi(t, first=False):
                if not first:
                    pool.wait_ge(hi_gathered, 16 * HI * t)
                pool.dma_start(ids_hi[:], ids[bass.ds(t * P, P), LO:FIELDS]).then_inc(hi_loaded, 16)

            def gather_lo(f):
                nc.gpsimd.indirect_dma_start(
                    out=rows[:, f * DIM:(f + 1) * DIM], out_offset=None, in_=tables[f],
                    in_offset=bass.IndirectOffsetOnAxis(ap=ids_lo[:, f:f + 1], axis=0),
                ).then_inc(lo_gathered, 16)

            def gather_hi(f):
                m = LO + f
                nc.gpsimd.indirect_dma_start(
                    out=rows[:, m * DIM:(m + 1) * DIM], out_offset=None, in_=tables[m],
                    in_offset=bass.IndirectOffsetOnAxis(ap=ids_hi[:, f:f + 1], axis=0),
                ).then_inc(hi_gathered, 16)

            def product(s, u, first, layer, c):
                i = pool_index(layer, c)
                if i == 0:
                    pool.wait_ge(x_ready[0], s + 1)
                if i == len(POOL_CHUNKS):
                    pool.wait_ge(x_ready[1], s + 1)
                if layer == L1 and c >= SPREAD:
                    pool.wait_ge(swap_done, SPREAD * s + c - SPREAD + 1)
                if not first or i >= POOL_RING:
                    pool.wait_ge(pool_used, POOL_STEP * s + last_in_buffer(i, POOL_RING, POOL_STEP) + 1)
                x = x1 if layer == L1 else x2
                nc.gpsimd.tensor_tensor(p_pool[:, i % POOL_RING, :], a_tile(u, layer, c), x[:],
                                        ALU.mult).then_inc(pool_made, 1)

            def products(s, u, first, n):
                layer = L1 if n < len(POOL_CHUNKS) else L2
                product(s, u, first, layer, POOL_CHUNKS[n % len(POOL_CHUNKS)])

            def even_step(s, t, first, hi, lo):
                if hi:
                    pool.wait_ge(hi_loaded, 16 * (t + 2))
                for n in range(POOL_STEP):
                    if lo and n == 2:
                        load_lo(t + 2)
                    if lo and n == LO_FROM:
                        pool.wait_ge(lo_loaded, 16 * (t + 3))
                        pool.wait_ge(turned, t + 2)
                    products(s, 0, first, n)
                    if hi:
                        for f in HI_AFTER[n]:
                            gather_hi(f)
                    if lo:
                        for f in LO_AFTER_EVEN[n]:
                            gather_lo(f)

            def odd_step(s, t, gather):
                for n in range(POOL_STEP):
                    products(s, 1, False, n)
                    if gather:
                        for f in LO_AFTER_ODD[n]:
                            gather_lo(f)
                        if n == 0:
                            load_hi(t + 2)

            load_lo(0, True)
            load_hi(0, True)
            pool.wait_ge(lo_loaded, 16)
            for f in range(LO):
                gather_lo(f)
            pool.wait_ge(hi_loaded, 16)
            for f in range(HI):
                gather_hi(f)
            load_lo(1)
            load_hi(1)
            pool.wait_ge(lo_loaded, 32)
            pool.wait_ge(turned, 1)
            for f in range(LO):
                gather_lo(f)
            even_step(0, 0, True, True, True)
            with pool.Fori(0, TILES - 3) as t:
                odd_step(2 * t + 1, t, True)
                even_step(2 * t + 2, t + 1, False, True, True)
            odd_step(2 * TILES - 5, TILES - 3, True)
            even_step(2 * TILES - 4, TILES - 2, False, True, False)
            odd_step(2 * TILES - 3, TILES - 2, False)
            even_step(2 * TILES - 2, TILES - 1, False, False, False)
            odd_step(2 * TILES - 1, TILES - 1, False)

        @block.scalar
        def _(act):
            def copy_x(t):
                act.wait_ge(turned, t + 1)
                nc.scalar.activation(x_tile, turned_x[:], ACT.Copy).then_inc(x_copied, 1)

            def relu_both_halves(x, n):
                for b in range(2):
                    for to, k, size in (0, 0, K), (K, K // 2, K // 2), (K + K // 2, 0, K // 2):
                        last = nc.scalar.activation(x[to:to + size, b * BLK:(b + 1) * BLK],
                                                    acc[n][b * K + k:b * K + k + size, :], ACT.Relu)
                last.then_inc(x_ready[n], 1)

            def swap(s, c, u_next, prepare_free):
                if prepare_free:
                    n = ORDER_L2.index((1, c))
                    if n in POOL_CHUNKS:
                        act.wait_ge(pool_made, POOL_STEP * s + pool_index(L2, n) + 1)
                    else:
                        act.wait_ge(dve_made, dve_before(s) + dve_index(L2, n, True) + 1)
                for half in range(2):
                    src = (1 - half) * K
                    last = nc.scalar.activation(swapped[half * K:(half + 1) * K, c, :],
                                                spread[src:src + K, u_next, c, :], ACT.Copy)
                last.then_inc(swap_done, 1)

            def relu0(s, u, first, before):
                act.wait_ge(dve_used, first_layer_from(s, first) + C0)
                relu_both_halves(x1, 0)
                if u == 0 and not first:
                    act.wait_ge(z_made, 3 * before - 2)
                nc.scalar.activation(out_l[:, 0, u, :], acc[0][:], ACT.Relu).then_inc(relu_done[0], 1)

            def relu1(s, u, before):
                act.wait_ge(dve_used, dve_before(s) + DVE_L)
                act.wait_ge(pool_used, POOL_STEP * s + len(POOL_CHUNKS))
                relu_both_halves(x2, 1)
                if before is not None:
                    act.wait_ge(z_made, 3 * before)
                nc.scalar.activation(out_l[:, 1, u, :], acc[1][:], ACT.Relu).then_inc(relu_done[1], 1)

            def relu2(s, u, prepare, before):
                act.wait_ge(dve_used, dve_before(s) + 2 * DVE_L + C0 * prepare)
                act.wait_ge(pool_used, POOL_STEP * (s + 1))
                if before is not None:
                    act.wait_ge(z_made, 3 * before)
                nc.scalar.activation(out_l[:, 2, u, :], acc[2][:], ACT.Relu).then_inc(relu_done[2], 1)

            def move_z(t):
                act.wait_ge(z_made, 3 * (t + 1))
                for to, k, n in (0, 0, 0), (K, 0, 1), (0, 1, 2):
                    last = nc.scalar.activation(z_moved[to:to + K, k, :], z[K - to:P - to, n, :], ACT.Copy)
                last.then_inc(z_moved_ready, 1)

            def mlp1(t, tiles):
                act.wait_ge(mlp_made, 3 * t + 1)
                act.wait_ge(x_stored, 32 * tiles)
                for n in range(H1 // P):
                    last = nc.scalar.activation(h1[:, n, :], mlp_acc[:, n * P:(n + 1) * P], ACT.Relu,
                                                bias=bt1[:, n:n + 1])
                last.then_inc(mlp_done, 1)

            def mlp2(t):
                act.wait_ge(mlp_made, 3 * t + 2)
                for n in range(H2 // P):
                    last = nc.scalar.activation(h2[:, n, :], mlp_acc[:, n * P:(n + 1) * P], ACT.Relu,
                                                bias=bt2[:, n:n + 1])
                last.then_inc(mlp_done, 1)

            def mlp3(t):
                act.wait_ge(mlp_made, 3 * t + 3)
                nc.scalar.activation(y_row[:], mlp_acc[0:1, 0:P], ACT.Copy).then_inc(mlp_done, 1)
                act.wait_ge(mlp_done, 3 * t + 3)
                act.dma_start(y[:, bass.ds(t * P, P)], y_row[:]).then_inc(y_stored, 16)

            def load_dense(t):
                act.dma_start(z_all[K:TOP, 1, :], dense_t[:, bass.ds(t * P, P)]).then_inc(dense_loaded, 16)

            def step(s, u, prepare, tile_before, this, turn=None):
                if tile_before is not None:
                    move_z(tile_before)
                    mlp1(tile_before, tile_before + 2)
                relu1(s, u, None if tile_before is None else tile_before + 1)
                if tile_before is not None:
                    mlp2(tile_before)
                    mlp3(tile_before)
                if prepare:
                    relu0(s + 1, 1 - u, False, None if this is None else this + 1)
                if this is not None:
                    load_dense(this)
                for c in range(SPREAD if prepare else 0):
                    swap(s, c, 1 - u, True)
                    if turn is not None and c == COPY_AFTER:
                        copy_x(turn)
                relu2(s, u, prepare, None if tile_before is None else tile_before + 1)
                if tile_before is not None:
                    act.wait_ge(y_stored, 16 * (tile_before + 1))

            act.wait_ge(w_loaded, LOADED)
            copy_x(0)
            relu0(0, 0, True, None)
            for c in range(SPREAD):
                swap(-1, c, 0, False)
            step(0, 0, True, None, None, 1)
            with act.Fori(0, TILES - 2) as t:
                step(2 * t + 1, 1, True, None, t)
                step(2 * t + 2, 0, True, t, None, t + 2)
            step(2 * TILES - 3, 1, True, None, TILES - 2)
            step(2 * TILES - 2, 0, True, TILES - 2, None)
            step(2 * TILES - 1, 1, False, None, TILES - 1)
            move_z(TILES - 1)
            mlp1(TILES - 1, TILES)
            mlp2(TILES - 1)
            mlp3(TILES - 1)
            act.wait_ge(y_stored, 16 * TILES)

        @block.vector
        def _(dve):
            def slots_free(s, u, first, prepare, layer, c, n):
                uses = [dve_last_use(u, prepare, first, layer, c + k) for k in range(n)]
                if any(use is not None for use in uses):
                    last = max(use for use in uses if use is not None)
                    dve.wait_ge(dve_used, dve_before(s) + last + 1)

            def over(x, n):
                return x.rearrange("p (o n) -> p o n", o=1).broadcast_to([x.shape[0], n, COLS])

            def products(s, u, first, prepare, layer, c, n):
                slots_free(s, u, first, prepare, layer, c, n)
                if c == 0:
                    dve.wait_ge(x_ready[(L1, L2).index(layer)], s + 1)
                if layer == L1 and c >= SPREAD:
                    dve.wait_ge(swap_done, SPREAD * s + c - SPREAD + n)
                x = x1 if layer == L1 else x2
                half_swapped, tile = (ORDER_L1 if layer == L1 else ORDER_L2)[c]
                tiles = swapped[:] if half_swapped else spread[:, u]
                to = dve_buffer(u, layer, c)
                nc.vector.tensor_tensor(p_dve[:, to:to + n, :], tiles[:, tile:tile + n, :],
                                        over(x[:], n), ALU.mult).then_inc(dve_made, n)

            def first_layer_products(s, u, at, c, n):
                rows_used = P if c < C0 - 1 else HALF
                to = dve_buffer(at, L0, c)
                if c == 0:
                    dve.wait_ge(q_loaded, 16 * (s + 1))
                    dve.wait_ge(spread_loaded[0], 16 * SHIFTS * (s + 1))
                if c == GROUP:
                    dve.wait_ge(spread_loaded[1], 16 * SHIFTS * (s + 1))
                nc.vector.tensor_tensor(p_dve[0:rows_used, to:to + n, :], spread[0:rows_used, u, c:c + n, :],
                                        over(q_tile[0:rows_used, :], n), ALU.mult).then_inc(dve_made, n)

            def sums(t, n):
                dve.wait_ge(relu_done[n], 2 * (t + 1))
                nc.vector.reduce_sum(z[:, n, :], out_l[:, n, :, :].rearrange("p u (d b) -> p b (u d)", b=P),
                                     AX_X).then_inc(z_made, 1)

            def fold(t):
                dve.wait_ge(z_moved_ready, t + 1)
                for to, k, n in (0, 0, 0), (K, 0, 1), (0, 1, 2):
                    last = nc.vector.tensor_tensor(z_all[to:to + K, k, :], z[to:to + K, n, :],
                                                   z_moved[to:to + K, k, :], ALU.add)
                last.then_inc(z_summed, 1)

            def step(s, u, first, prepare, this, before):
                for c, n in DVE_GROUPS:
                    products(s, u, first, prepare, L1, c, n)
                    if c == SUM1_AFTER and before is not None:
                        sums(before, 1)
                    if c == SUM_AFTER and before is not None:
                        sums(before, 2)
                    if c == FOLD_AFTER and before is not None:
                        fold(before)
                    if c == SUM_AFTER and this is not None:
                        sums(this, 0)
                if prepare:
                    for c, n in (0, 3), (3, 1), (4, 1):
                        slots_free(s, u, first, prepare, L0, c, n)
                        first_layer_products(s + 1, 1 - u, u, c, n)
                for c, n in DVE_GROUPS_L2:
                    products(s, u, first, prepare, L2, c, n)

            dve.wait_ge(w_loaded, LOADED)
            for part in (w0_s[FIELDS:K, 0, :], w0_b[FIELDS:K, 0, :]), (w0_s[K:, 0, :], w0_b[K:, 0, :]), \
                    (w0_s[:, 1:C0 - 1, :], w0_b[:, 1:, :]), (w0_s[0:HALF, C0 - 1, :], w0_lb[:]):
                nc.vector.tensor_tensor(part[0], part[0], part[1], ALU.add).then_inc(w0_ready, 1)
            for c, n in (0, 1), (1, 1), (2, 1), (3, 1), (4, 1):
                first_layer_products(0, 0, 1, c, n)
            step(0, 0, True, True, None, None)
            with dve.Fori(0, TILES - 1) as t:
                step(2 * t + 1, 1, False, True, t, None)
                step(2 * t + 2, 0, False, True, None, t)
            step(2 * TILES - 1, 1, False, False, TILES - 1, None)
            sums(TILES - 1, 1)
            sums(TILES - 1, 2)
            fold(TILES - 1)

        @block.tensor
        def _(pe):
            def turn(t):
                pe.wait_ge(lo_gathered, 16 * LO * (t + 1))
                pe.wait_ge(hi_gathered, 16 * HI * (t + 1))
                for j in range(TURNS):
                    last = nc.tensor.transpose(turned_x[:, j, :], rows[:, j * P:(j + 1) * P], idn[:])
                last.then_inc(turned, 1)

            def contract(n, w, prod, start, stop):
                for b in range(2):
                    last = nc.tensor.matmul(acc[n][b * K:(b + 1) * K, :], w,
                                            prod[:, b * BLK:(b + 1) * BLK], start=start, stop=stop)
                return last

            def chunk(s, u, prepare, layer, c):
                n, w = (1, w1_s[:, c, :]) if layer == L1 else (2, w2_s[:, c, :])
                if c == 0:
                    pe.wait_ge(relu_done[n], s)
                if c in POOL_CHUNKS:
                    i = pool_index(layer, c)
                    pe.wait_ge(pool_made, POOL_STEP * s + i + 1)
                    contract(n, w, p_pool[:, i % POOL_RING, :], c == 0, c == C1 - 1
                             ).then_inc(pool_used, 1)
                else:
                    i = dve_index(layer, c, prepare)
                    pe.wait_ge(dve_made, dve_before(s) + i + 1)
                    contract(n, w, p_dve[:, dve_buffer(u, layer, c), :], c == 0, c == C1 - 1
                             ).then_inc(dve_used, 1)

            def first_layer_chunk(s, u, first, c):
                n = P if c < C0 - 1 else HALF
                if c == 0 and not first:
                    pe.wait_ge(relu_done[0], s)
                pe.wait_ge(dve_made, first_layer_from(s, first) + c + 1)
                contract(0, w0_s[0:n, c, :], p_dve[0:n, dve_buffer(u, L0, c), :], c == 0, c == C0 - 1
                         ).then_inc(dve_used, 1)

            def mlp1(t):
                pe.wait_ge(z_summed, t + 1)
                pe.wait_ge(dense_loaded, 16 * (t + 1))
                for n in range(H1 // P):
                    cols = slice(n * P, (n + 1) * P)
                    nc.tensor.matmul(mlp_acc[:, cols], wt1[:, 0, cols], z_all[:, 0, :],
                                     start=True, stop=False)
                    last = nc.tensor.matmul(mlp_acc[:, cols], wt1[0:TOP, 1, cols], z_all[0:TOP, 1, :],
                                            start=False, stop=True)
                last.then_inc(mlp_made, 1)

            def mlp2(t):
                pe.wait_ge(mlp_done, 3 * t + 1)
                for n in range(H2 // P):
                    cols = slice(n * P, (n + 1) * P)
                    for k in range(H1 // P):
                        last = nc.tensor.matmul(mlp_acc[:, cols], wt2[:, k, cols], h1[:, k, :],
                                                start=(k == 0), stop=(k == H1 // P - 1))
                last.then_inc(mlp_made, 1)

            def mlp3(t):
                pe.wait_ge(mlp_done, 3 * t + 2)
                for k in range(H2 // P):
                    last = nc.tensor.matmul(mlp_acc[0:1, 0:P], wt3[:, k:k + 1], h2[:, k, :],
                                            start=(k == 0), stop=(k == H2 // P - 1))
                last.then_inc(mlp_made, 1)

            def step(s, u, prepare, before=None, turns=None):
                for c in range(C1):
                    chunk(s, u, prepare, L1, c)
                    if prepare:
                        if before is not None and c == MLP1_AFTER:
                            mlp1(before)
                if prepare:
                    for c in range(C0):
                        first_layer_chunk(s + 1, u, False, c)
                        if before is not None and c == MLP2_AFTER:
                            mlp2(before)
                        if before is not None and c == MLP3_AFTER:
                            mlp3(before)
                for c in range(C1):
                    chunk(s, u, prepare, L2, c)
                    if turns is not None and c == TURN_AFTER:
                        turn(turns)

            pe.wait_ge(w_loaded, LOADED)
            turn(0)
            pe.wait_ge(w0_ready, 4)
            for c in range(C0):
                first_layer_chunk(0, 1, True, c)
            step(0, 0, True, turns=1)
            with pe.Fori(0, TILES - 2) as t:
                step(2 * t + 1, 1, True)
                step(2 * t + 2, 0, True, before=t, turns=t + 2)
            step(2 * TILES - 3, 1, True)
            step(2 * TILES - 2, 0, True, before=TILES - 2)
            step(2 * TILES - 1, 1, False)
            mlp1(TILES - 1)
            mlp2(TILES - 1)
            mlp3(TILES - 1)


def pairs():
    delta, m = np.divmod(np.arange(FIELDS * HALF), FIELDS)
    delta = np.concatenate([delta, np.full(HALF, HALF)])
    m = np.concatenate([m, np.arange(HALF)])
    return m, (m + delta) % FIELDS


def spread_rows(order):
    p = np.arange(P)
    h = np.where(p < K, p, (p + K // 2) % K)
    chunks = [(p + SHIFTS * c + (p // FIELDS + half_swapped * SHIFTS // 2) % SHIFTS) % FIELDS * K + h
              for half_swapped, c in order]
    return np.concatenate(chunks)


def kernel(**inputs):
    import concourse.bacc as bacc
    from concourse.bass_utils import run_bass_kernel_spmd

    raw = {k: np.asarray(v) for k, v in inputs.items()}
    m, h = pairs()
    w0 = raw["L0_rec_W0"]
    arrays = {"ids": raw["ids"]}
    arrays.update({f"tbl_{f}": raw[f"tbl_{f}"] for f in range(FIELDS)})
    arrays.update(
        dense_t=raw["dense_ctx"].T, w0_mh=w0[m, h], w0_hm=w0[h, m],
        w1=raw["L0_rec_W1"].reshape(FIELDS * K, K)[spread_rows(ORDER_L1)], w2=raw["L0_rec_W2"].reshape(FIELDS * K, K)[spread_rows(ORDER_L2)],
        w_top1=raw["W_top1"], b_top1=raw["b_top1"].reshape(H1 // P, P).T,
        w_top2=raw["W_top2"], b_top2=raw["b_top2"].reshape(H2 // P, P).T,
        w_top3=raw["W_top3"].reshape(H2 // P, P).T,
        ident=np.eye(P, dtype=np.float32),
    )
    arrays = {f"in_{k}": np.ascontiguousarray(v) for k, v in arrays.items()}

    nc = bacc.Bacc("TRN2", target_bir_lowering=False, num_devices=1)
    aps = {k[3:]: nc.dram_tensor(k, v.shape, mybir.dt.from_np(v.dtype), kind="ExternalInput").ap()
           for k, v in arrays.items()}
    tables = [aps.pop(f"tbl_{f}") for f in range(FIELDS)]
    y = nc.dram_tensor("y", (1, BATCH), F32, kind="ExternalOutput").ap()
    scratch = nc.dram_tensor("x0_of_tiles", (TILES, X_ROWS, DIM * P), F32, kind="Internal").ap()
    build_kernel(nc, tables=tables, scratch=scratch, y=y, **aps)
    result = run_bass_kernel_spmd(nc, [arrays], core_ids=[0])
    return result.results[0]["y"].reshape(BATCH, 1)
```
